# Optimizing a Trainium2 kernel written in Bass

```python
import numpy as np
import jax
import jax.numpy as jnp

def _softmax(x, axis=-1):
    return jax.nn.softmax(x, axis=axis)

def _gelu(x):
    return jax.nn.gelu(x, approximate=True)

def _silu(x):
    return jax.nn.silu(x)

def _sigmoid(x):
    return jax.nn.sigmoid(x)

def _layernorm(x, axis=-1, eps=1e-05):
    m = jnp.mean(x, axis=axis, keepdims=True)
    v = jnp.var(x, axis=axis, keepdims=True)
    return (x - m) / jnp.sqrt(v + eps)

def _scatter_add(tgt, idx, src, axis=0):
    return tgt.at[idx].add(src)

def _segment_sum(src, seg, n):
    return jax.ops.segment_sum(src, seg, n)
kernel_name = 'mk_lm_tower_d1_tok_ids512_r4_99c064'

def setup_inputs(seed: int=0):
    np.random.seed(seed)
    _w = jnp.asarray

    def _rec_inputs():
        import jax
        import jax.numpy as jnp
        _rk = jax.random.key(seed)
        x = jax.random.randint(jax.random.fold_in(_rk, 1), (4, 512), 0, 12564, jnp.int32)
        return x
    x = _rec_inputs()

    def _L0_tok_setup():
        import jax, jax.numpy as jnp
        import numpy as np
        VOCAB = 50257
        PROJ_DIM = 128
        B, S = (8, 1024)
        key = jax.random.key(seed)
        kx, kw = jax.random.split(key)
        x = jax.random.randint(kx, (B, S), 0, VOCAB)
        W = jax.random.normal(kw, (PROJ_DIM, VOCAB), dtype=jnp.float32) * 0.02
        return {'x': x, 'W': W}
    _L0_tok_all = _L0_tok_setup()
    _L0_tok_in = {k: v for k, v in _L0_tok_all.items() if k in ('W',)}
    del _L0_tok_all

    def _L0_attn_setup():
        import jax, jax.numpy as jnp
        import numpy as np
        BATCH, SEQ, DIN, H, DOUT = (8, 512, 128, 128, 128)

        def _ssm(x, A, B, C):
            xb = jnp.einsum('btd,hd->bth', x, B)
            s0 = jnp.zeros((x.shape[0], A.shape[0]), dtype=x.dtype)

            def step(s, xb_t):
                s = jnp.tanh(s @ A.T + xb_t)
                return (s, s)
            _, states = jax.lax.scan(step, s0, jnp.swapaxes(xb, 0, 1))
            states = jnp.swapaxes(states, 0, 1)
            return jnp.einsum('bth,oh->bto', states, C)
        key = jax.random.key(seed)
        ks = jax.random.split(key, 8)
        s = 1.0 / np.sqrt(H)
        return {'x': jax.random.normal(ks[0], (BATCH, SEQ, DIN), dtype=jnp.float32), 'A': jax.random.normal(ks[1], (H, H), dtype=jnp.float32) * s, 'B': jax.random.normal(ks[2], (H, DIN), dtype=jnp.float32) * s, 'C': jax.random.normal(ks[3], (H, H), dtype=jnp.float32) * s, 'Wg': jax.random.normal(ks[4], (H, H), dtype=jnp.float32) * s, 'bg': jnp.zeros((H,), dtype=jnp.float32), 'Wo': jax.random.normal(ks[5], (DOUT, H), dtype=jnp.float32) * s, 'bo': jnp.zeros((DOUT,), dtype=jnp.float32)}
    _L0_attn_all = _L0_attn_setup()
    _L0_attn_in = {k: v for k, v in _L0_attn_all.items() if k in ('A', 'B', 'C', 'Wg', 'bg', 'Wo', 'bo')}
    del _L0_attn_all

    def _L0_ffn_setup():
        import jax, jax.numpy as jnp
        import numpy as np
        E = 8
        K = 1
        D = 128
        I = 512
        B, T = (2, 512)
        key = jax.random.key(seed)
        ks = jax.random.split(key, 7)
        s = 0.02
        x = jax.random.normal(ks[0], (B, T, D), jnp.float32)
        gate_w = jax.random.normal(ks[1], (E, D), jnp.float32) * s
        w1 = jax.random.normal(ks[2], (E, I, D), jnp.float32) * s
        w2 = jax.random.normal(ks[3], (E, D, I), jnp.float32) * s
        w3 = jax.random.normal(ks[4], (E, I, D), jnp.float32) * s
        sw1 = jax.random.normal(ks[5], (I, D), jnp.float32) * s
        sw2 = jax.random.normal(ks[6], (D, I), jnp.float32) * s
        return {'x': x, 'gate_w': gate_w, 'w1': w1, 'w2': w2, 'w3': w3, 'sw1': sw1, 'sw2': sw2}
    _L0_ffn_all = _L0_ffn_setup()
    _L0_ffn_in = {k: v for k, v in _L0_ffn_all.items() if k in ('gate_w', 'w1', 'w2', 'w3', 'sw1', 'sw2')}
    del _L0_ffn_all
    return {'x': x, 'L0_tok_W': _L0_tok_in['W'], 'L0_attn_A': _L0_attn_in['A'], 'L0_attn_B': _L0_attn_in['B'], 'L0_attn_C': _L0_attn_in['C'], 'L0_attn_Wg': _L0_attn_in['Wg'], 'L0_attn_bg': _L0_attn_in['bg'], 'L0_attn_Wo': _L0_attn_in['Wo'], 'L0_attn_bo': _L0_attn_in['bo'], 'L0_ffn_gate_w': _L0_ffn_in['gate_w'], 'L0_ffn_w1': _L0_ffn_in['w1'], 'L0_ffn_w2': _L0_ffn_in['w2'], 'L0_ffn_w3': _L0_ffn_in['w3'], 'L0_ffn_sw1': _L0_ffn_in['sw1'], 'L0_ffn_sw2': _L0_ffn_in['sw2']}

def reference(x, L0_tok_W, L0_attn_A, L0_attn_B, L0_attn_C, L0_attn_Wg, L0_attn_bg, L0_attn_Wo, L0_attn_bo, L0_ffn_gate_w, L0_ffn_w1, L0_ffn_w2, L0_ffn_w3, L0_ffn_sw1, L0_ffn_sw2):
    import jax
    import jax.numpy as jnp

    def _L0_tok_ref(x, W):
        import jax, jax.numpy as jnp
        import numpy as np
        VOCAB = 50257
        PROJ_DIM = 128
        B, S = (8, 1024)
        return jnp.take(W.T, x, axis=0)

    def _L0_attn_ref(x, A, B, C, Wg, bg, Wo, bo):
        import jax, jax.numpy as jnp
        import numpy as np
        BATCH, SEQ, DIN, H, DOUT = (8, 512, 128, 128, 128)

        def _ssm(x, A, B, C):
            xb = jnp.einsum('btd,hd->bth', x, B)
            s0 = jnp.zeros((x.shape[0], A.shape[0]), dtype=x.dtype)

            def step(s, xb_t):
                s = jnp.tanh(s @ A.T + xb_t)
                return (s, s)
            _, states = jax.lax.scan(step, s0, jnp.swapaxes(xb, 0, 1))
            states = jnp.swapaxes(states, 0, 1)
            return jnp.einsum('bth,oh->bto', states, C)
        h = _ssm(x, A, B, C)
        gated = jax.nn.sigmoid(jnp.einsum('bth,gh->btg', h, Wg) + bg) * h
        return jnp.einsum('bth,oh->bto', gated, Wo) + bo

    def _L0_ffn_ref(x, gate_w, w1, w2, w3, sw1, sw2):
        import jax, jax.numpy as jnp
        import numpy as np
        E = 8
        K = 1
        D = 128
        I = 512
        B, T = (2, 512)
        xf = x.reshape(-1, D)
        logits = xf @ gate_w.T
        wts, idx = jax.lax.top_k(logits, K)
        wts = jax.nn.softmax(wts, axis=-1)
        comb = jnp.einsum('nke,nk->ne', jax.nn.one_hot(idx, E, dtype=xf.dtype), wts)
        h = jax.nn.silu(jnp.einsum('nd,eid->nei', xf, w1)) * jnp.einsum('nd,eid->nei', xf, w3)
        y = jnp.einsum('nei,edi->nd', h * comb[:, :, None], w2)
        y = y + jax.nn.gelu(xf @ sw1.T, approximate=False) @ sw2.T
        return y.reshape(x.shape)
    h = _L0_tok_ref(x, L0_tok_W)
    h = h + _L0_attn_ref(_layernorm(h, axis=-1), L0_attn_A, L0_attn_B, L0_attn_C, L0_attn_Wg, L0_attn_bg, L0_attn_Wo, L0_attn_bo)
    h = h + _L0_ffn_ref(_layernorm(h, axis=-1), L0_ffn_gate_w, L0_ffn_w1, L0_ffn_w2, L0_ffn_w3, L0_ffn_sw1, L0_ffn_sw2)
    return h

_drawn_inputs = setup_inputs


def setup_inputs(seed=0):
    import zlib

    import numpy as np

    out = dict(_drawn_inputs(seed))
    spreads = {'L0_attn_bg': (0.0, 0.1), 'L0_attn_bo': (0.0, 0.1)}
    factors = {}
    for name, (base, spread) in spreads.items():
        noise = np.random.default_rng([zlib.crc32(name.encode()), seed]).standard_normal(out[name].shape)
        drawn = base * np.exp(spread * noise) if base else spread * noise
        out[name] = jnp.asarray(drawn.astype(out[name].dtype))
    for name, factor in factors.items():
        out[name] = (out[name] * factor).astype(out[name].dtype)
    return out
```

```python
from contextlib import ExitStack

import numpy as np
import concourse.bass as bass
from concourse import mybir

P = 128
BATCH, SEQ = 4, 512
EXPERTS, INNER = 8, 512
CHUNK = 32
CHUNKS = SEQ // CHUNK
WARM = 48
COLS = CHUNKS * BATCH
PADC = 2 * BATCH
XW = COLS + PADC
STEPS = WARM + CHUNK
MAIN = (1 + WARM) * COLS
TILES = BATCH * SEQ // P
GROUPS = TILES // 4
GC = 4 * P
IC = INNER // P
BLOCKS = TILES + EXPERTS - 1
ROW = P + 2
NO_ROW = 4096
EPS = 1e-5
TOL = 2.0 ** -18

F32 = mybir.dt.float32
I32 = mybir.dt.int32
ALU = mybir.AluOpType
ACT = mybir.ActivationFunctionType
AX = mybir.AxisListType

C_IDENT, C_RANK, C_ONES, C_REV, C_CARRY, C_BLOCK, C_EPS, C_POW = 0, 128, 256, 384, 512, 640, 824, 840
C_END = 856


def shape_constants():
    c = np.zeros((P, C_END), np.float32)
    j = np.arange(P)
    c[:, C_IDENT:C_IDENT + P] = np.eye(P)
    c[:, C_RANK:C_RANK + P] = -(j[:, None] >= j[None, :]).astype(np.float32)
    c[:, C_ONES:C_ONES + P] = 1.0
    c[:, C_REV:C_REV + P] = np.tile(EXPERTS - np.arange(EXPERTS), TILES)
    c[:, C_CARRY:C_CARRY + P] = np.tile(np.arange(TILES) > 0, EXPERTS)
    c[:, C_BLOCK:C_BLOCK + BLOCKS * EXPERTS] = np.repeat(np.arange(BLOCKS), EXPERTS)
    c[:, C_EPS:C_EPS + TILES] = EPS
    c[:, C_POW:C_POW + TILES] = -0.5
    return c


def row_ids():
    q, t = np.arange(P)[:, None], np.arange(TILES)[None, :]
    pos = (q // BATCH % CHUNKS) * CHUNK + 2 * t + q // COLS
    return np.stack([(q % BATCH) * SEQ + pos, t * P + q], -1).astype(np.int32)


def build(nc, tok, ids, consts, emb, sq, bg, bo, gate, w1, w3, w2, sw1, sw2, out, dispatch, resid):
    with ExitStack() as ctx:
        def sb(name, shape, dt=F32):
            return ctx.enter_context(nc.sbuf_tensor(name, shape, dt))

        def sem(name):
            return ctx.enter_context(nc.semaphore(name))

        bank = [ctx.enter_context(nc.psum_tensor(f"bank{i}", [P, 512], F32)) for i in range(8)]

        tok_sb = sb("tok_sb", [P, TILES], I32)
        cst = sb("cst", [P, C_END])
        sq_sb = sb("sq_sb", [P, 5, P])
        bg_sb = sb("bg_sb", [P, 1])
        half_bg = sb("half_bg", [P, 1])
        bo_sb = sb("bo_sb", [P, P])
        gate_sb = sb("gate_sb", [P, EXPERTS])
        w1_sb = sb("w1_sb", [P, EXPERTS * INNER])
        w3_sb = sb("w3_sb", [P, EXPERTS * INNER])
        w2_sb = sb("w2_sb", [P, EXPERTS * INNER])
        sw1_sb = sb("sw1_sb", [P, INNER])
        sw2_sb = sb("sw2_sb", [P, IC, P])
        ident = cst[:, C_IDENT:C_IDENT + P]
        ones = cst[:, C_ONES:C_ONES + P]
        at, bt, ct, wgt, wot = (sq_sb[:, i, :] for i in range(5))

        emb_rows = sb("emb_rows", [P, TILES, P])
        stats = sb("stats", [P, TILES, 6])
        meanvar = sb("meanvar", [P, TILES, 2])
        vareps = sb("vareps", [P, TILES])
        rstd = sb("rstd", [P, TILES])
        norm_rows = sb("norm_rows", [P, TILES, P])
        x_in = sb("x_in", [P, CHUNK * XW])

        states = sb("states", [P, (1 + STEPS) * COLS])
        piece = sb("piece", [P, CHUNK, BATCH])
        diff = sb("diff", [P, COLS - BATCH])
        diff2 = sb("diff2", [P, COLS - BATCH])
        close = sb("close", [P, COLS - BATCH])
        close_row = sb("close_row", [P, 1])
        agree = sb("agree", [1, 1])
        agree_i = sb("agree_i", [1, 1], I32)

        resid_bo = sb("resid_bo", [P, TILES, P])
        hid = sb("hid", [P, 2, GC])
        gate_t = sb("gate_t", [P, 2, GC])
        gated = sb("gated", [P, 2, GC])
        attn_out = sb("attn_out", [P, TILES, P])
        stats2 = sb("stats2", [P, TILES, 6])
        meanvar2 = sb("meanvar2", [P, TILES, 2])
        vareps2 = sb("vareps2", [P, TILES])
        rstd2 = sb("rstd2", [P, TILES])
        rows = sb("rows", [P, TILES, ROW])
        x_ffn = sb("x_ffn", [P, TILES * P])

        ET = EXPERTS * TILES
        top = sb("top", [P, TILES])
        is_top = sb("is_top", [P, ET])
        rev_top = sb("rev_top", [P, ET])
        first_rev = sb("first_rev", [P, TILES])
        onehot = sb("onehot", [P, ET])
        upto = sb("upto", [P, ET])
        place = sb("place", [P, ET])
        place_all = sb("place_all", [P, ET])
        place_own = sb("place_own", [P, ET])
        blocks_i0 = sb("blocks_i0", [P, EXPERTS], I32)
        blocks_i = sb("blocks_i", [P, EXPERTS], I32)
        blocks_end = sb("blocks_end", [P, EXPERTS])
        blocks_start = sb("blocks_start", [P, EXPERTS])
        slot_f = sb("slot_f", [P, TILES])
        slot_i = sb("slot_i", [P, TILES], I32)
        past = sb("past", [1, BLOCKS * EXPERTS])
        block_expert_f = sb("block_expert_f", [1, BLOCKS])
        block_expert = sb("block_expert", [1, BLOCKS], I32)
        fill = sb("fill", [P, ROW])
        ids_all = sb("ids_all", [P, BLOCKS, 2])

        act_sh = sb("act_sh", [P, 2, IC, GC])
        base = sb("base", [P, TILES, P])

        xblk = sb("xblk", [P, 2, P])
        xblk_t = sb("xblk_t", [P, 2, P])
        silu = sb("silu", [P, 2, INNER])
        prod = sb("prod", [P, 2, INNER])
        prod_t = sb("prod_t", [P, 2, INNER])
        idb = [sb(f"idb{i}", [P, 2], I32) for i in range(2)]
        res_blk = [sb(f"res_blk{i}", [P, P]) for i in range(2)]
        out_blk = [sb(f"out_blk{i}", [P, P]) for i in range(2)]

        tok_in, small_in, weights_in = sem("tok_in"), sem("small_in"), sem("weights_in")
        sh_weights_in = sem("sh_weights_in")
        ids_in, filled, fill_stored = sem("ids_in"), sem("filled"), sem("fill_stored")
        gathered = [sem(f"gathered{g}") for g in range(GROUPS)]
        dve_step, pool_step = sem("dve_step"), sem("pool_step")
        var_ready, rstd_ready, norm_ready = sem("var_ready"), sem("rstd_ready"), sem("norm_ready")
        norm_turned, x_ready, pads_zero = sem("norm_turned"), sem("x_ready"), sem("pads_zero")
        pre_ready, state_ready = sem("pre_ready"), sem("state_ready")
        close_ready, close_turned, agree_ready = sem("close_ready"), sem("close_turned"), sem("agree_ready")
        seq_pre, seq_state, seq_kept = sem("seq_pre"), sem("seq_state"), sem("seq_kept")
        bg_ready, resid_ready = sem("bg_ready"), sem("resid_ready")
        c_done, hid_ready, wg_done, tanh_ready, gated_ready, wo_done, attn_ready = (
            sem(n) for n in ("c_done", "hid_ready", "wg_done", "tanh_ready", "gated_ready", "wo_done", "attn_ready"))
        var2_ready, rstd2_ready, rows_ready, rows_turned, xffn_ready, logits_done = (
            sem(n) for n in ("var2_ready", "rstd2_ready", "rows_ready", "rows_turned", "xffn_ready", "logits_done"))
        onehot_ready, counts_done, slots_ready, experts_ready = (
            sem(n) for n in ("onehot_ready", "counts_done", "slots_ready", "experts_ready"))
        dispatched = sem("dispatched")
        up_done, gelu_done, down_done, base_ready, base_stored = (
            sem(n) for n in ("up_done", "gelu_done", "down_done", "base_ready", "base_stored"))
        all_ids_in = sem("all_ids_in")
        xblk_in = [sem(f"xblk_in{i}") for i in range(2)]
        res_in = [sem(f"res_in{i}") for i in range(2)]
        out_stored = [sem(f"out_stored{i}") for i in range(2)]
        id_copied, blk_turned, xt_ready, h_done, silu_ready, prod_ready, prod_turned, prodt_ready, y_done, outb_ready = (
            sem(n) for n in ("id_copied", "blk_turned", "xt_ready", "h_done", "silu_ready", "prod_ready",
                             "prod_turned", "prodt_ready", "y_done", "outb_ready"))
        res_zero, first_id_copied = sem("res_zero"), sem("first_id_copied")

        block = ctx.enter_context(nc.Block())

        def pipelined(eng, body, lag):
            lo = 4
            hi = lo + (BLOCKS - lo) // 2 * 2
            for k in range(lo):
                body(k, k % 2, k)
            with eng.Fori(0, (hi - lo) // 2) as m:
                for u in range(2):
                    body(m * 2 + (lo + u), u, None)
            for k in range(hi, BLOCKS + lag):
                body(k, k % 2, k)

        def pair_count(k, u, unit):
            return (k - u) * (unit // 2) + unit

        @block.sync
        def _(sp):
            sp.dma_start(tok_sb[:], tok).then_inc(tok_in, 16)
            sp.dma_start(cst[:], consts).then_inc(small_in, 16)
            sp.dma_start(sq_sb[:], sq).then_inc(small_in, 16)
            sp.dma_start(bg_sb[:], bg).then_inc(small_in, 16)
            sp.dma_start(bo_sb[:], bo.to_broadcast([P, P])).then_inc(small_in, 16)
            sp.dma_start(gate_sb[:], gate).then_inc(small_in, 16)
            sp.dma_start(rows[:].bitcast(I32)[:, :, P:ROW], ids).then_inc(ids_in, 16)
            sp.wait_ge(filled, 2)
            sp.dma_start(dispatch.rearrange("(k p) c -> p k c", p=P),
                         fill[:].unsqueeze(1).to_broadcast([P, BLOCKS, ROW])).then_inc(fill_stored, 16)
            sp.dma_start(sw1_sb[:], sw1).then_inc(sh_weights_in, 16)
            sp.dma_start(sw2_sb[:], sw2).then_inc(sh_weights_in, 16)
            sp.dma_start(w1_sb[:], w1).then_inc(weights_in, 16)
            sp.dma_start(w3_sb[:], w3).then_inc(weights_in, 16)
            sp.dma_start(w2_sb[:], w2).then_inc(weights_in, 16)
            sp.wait_ge(dispatched, 16 * TILES)
            sp.dma_start(ids_all[:], dispatch.rearrange("(k p) c -> p k c", p=P)[:, :, P:ROW]).then_inc(all_ids_in, 16)

            def load_block(k, u, static):
                if static is None or static >= 2:
                    sp.wait_ge(blk_turned, k - 1)
                sp.dma_start(xblk[:, u, :], dispatch[bass.ds(k * P, P), 0:P]).then_inc(xblk_in[u], 16)

            for k in range(2):
                load_block(k, k, k)
            for g in range(GROUPS):
                sp.wait_ge(base_ready, g + 1)
                sp.dma_start(resid.rearrange("(t p) d -> p t d", p=P)[:, 4 * g:4 * g + 4, :],
                             base[:, 4 * g:4 * g + 4, :]).then_inc(base_stored, 16)
            with sp.Fori(0, (BLOCKS - 3) // 2) as m:
                for u in range(2):
                    load_block(m * 2 + (2 + u), u, None)
            load_block(BLOCKS - 1, (BLOCKS - 1) % 2, BLOCKS - 1)
            for u in range(2):
                sp.wait_ge(out_stored[u], 16 * len(range(u, BLOCKS, 2)))

        @block.gpsimd
        def _(pool):
            pool.wait_ge(tok_in, 16)
            for t in range(TILES):
                pool.indirect_dma_start(out=emb_rows[:, t, :], out_offset=None, in_=emb,
                                        in_offset=bass.IndirectOffsetOnAxis(ap=tok_sb[:, t:t + 1], axis=0),
                                        ).then_inc(gathered[t // 4], 16)
            pool.memset(fill[:, 0:P], 0.0).then_inc(filled, 1)
            pool.memset(fill[:].bitcast(I32)[:, P:ROW], NO_ROW).then_inc(filled, 1)
            pool.wait_ge(small_in, 80)
            for g in range(GROUPS):
                ts = slice(4 * g, 4 * g + 4)
                pool.wait_ge(var_ready, g + 1)
                pool.tensor_tensor(rstd[:, ts], vareps[:, ts], cst[:, C_POW:C_POW + 4], ALU.pow).then_inc(rstd_ready, 1)
            for g in range(GROUPS):
                ts = slice(4 * g, 4 * g + 4)
                pool.tensor_tensor(resid_bo[:, ts, :], emb_rows[:, ts, :],
                                   bo_sb[:].unsqueeze(1).to_broadcast([P, 4, P]), ALU.add).then_inc(resid_ready, 1)
            for i in range(2):
                pool.memset(res_blk[i][:], 0.0).then_inc(res_zero, 1)
            for g in range(GROUPS):
                ts = slice(4 * g, 4 * g + 4)
                pool.wait_ge(var2_ready, g + 1)
                pool.tensor_tensor(rstd2[:, ts], vareps2[:, ts], cst[:, C_POW:C_POW + 4], ALU.pow).then_inc(rstd2_ready, 1)
            pool.wait_ge(fill_stored, 16)
            pool.wait_ge(ids_in, 16)
            pool.wait_ge(rows_ready, TILES)
            pool.wait_ge(slots_ready, 1)
            for t in range(TILES):
                pool.indirect_dma_start(out=dispatch, out_offset=bass.IndirectOffsetOnAxis(ap=slot_i[:, t:t + 1], axis=0),
                                        in_=rows[:, t, :], in_offset=None).then_inc(dispatched, 16)
            pool.wait_ge(all_ids_in, 16)
            pool.wait_ge(res_zero, 2)
            last_row = pool.to_reg(TILES * P - 1)

            def step(k, u, static):
                if static is None or static < BLOCKS:
                    if static is None or static >= 2:
                        pool.wait_ge(out_stored[u], pair_count(k - 2, u, 16))
                    pool.tensor_copy(idb[u][:], ids_all[:].bitcast(I32).rearrange("p k c -> p (k c)")[:, bass.ds(k * 2, 2)]
                                     ).then_inc(first_id_copied if static == 0 else id_copied, 1)
                    pool.wait_ge(base_stored, 16 * GROUPS)
                    if static == 0:
                        pool.wait_ge(first_id_copied, 1)
                    else:
                        pool.wait_ge(id_copied, k)
                    pool.indirect_dma_start(out=res_blk[u][:], out_offset=None, in_=resid,
                                            in_offset=bass.IndirectOffsetOnAxis(ap=idb[u][:, 1:2], axis=0),
                                            bounds_check=last_row, oob_is_err=False).then_inc(res_in[u], 16)
                if static is None or static >= 1:
                    pool.wait_ge(all_ids_in, 16)
                    pool.wait_ge(outb_ready, k)
                    pool.indirect_dma_start(out=out, out_offset=bass.IndirectOffsetOnAxis(ap=idb[1 - u][:, 0:1], axis=0),
                                            in_=out_blk[1 - u][:], in_offset=None,
                                            bounds_check=last_row, oob_is_err=False).then_inc(out_stored[1 - u], 16)

            pipelined(pool, step, 1)

        @block.tensor
        def _(pe):
            pe.wait_ge(small_in, 80)
            for g in range(GROUPS):
                if g >= 2:
                    pe.wait_ge(x_ready, g - 1)
                for i in range(4):
                    t = 4 * g + i
                    pe.wait_ge(norm_ready, t + 1)
                    mm = pe.transpose(bank[g % 2][:, i * P:(i + 1) * P], norm_rows[:, t, :], ident)
                mm.then_inc(norm_turned, 1)
            pe.wait_ge(x_ready, GROUPS)
            pe.wait_ge(pads_zero, 1)

            for i in range(STEPS):
                shift = -((i - WARM) // CHUNK)
                p = (i - WARM) % CHUNK
                x_at = p * XW + PADC - shift * BATCH
                pre = bank[i % 2][:, 0:COLS]
                pe.matmul(pre, bt, x_in[:, x_at:x_at + COLS], start=True, stop=False)
                pe.wait_ge(state_ready, i + 1)
                pe.matmul(pre, at, states[:, i * COLS:(i + 1) * COLS], start=False, stop=True).then_inc(pre_ready, 1)

            pe.wait_ge(close_ready, 1)
            pe.transpose(bank[2][0:1, 0:P], close_row[:, 0:1], ident).then_inc(close_turned, 1)
            pe.wait_ge(agree_ready, 1)
            ok = pe.value_load(agree_i[0:1, 0:1], min_val=0, max_val=1)
            with pe.If(ok == 0):
                with pe.Fori(0, CHUNKS) as c:
                    for p in range(CHUNK):
                        pre = bank[p % 2][:, 0:BATCH]
                        pe.matmul(pre, bt, x_in[:, bass.ds(c * BATCH + (p * XW + PADC), BATCH)], start=True, stop=False)
                        pe.wait_ge(seq_state, c * CHUNK + (p + 1))
                        pe.matmul(pre, at, piece[:, (p - 1) % CHUNK, :], start=False, stop=True).then_inc(seq_pre, 1)
                pe.wait_ge(seq_kept, CHUNKS)

            pe.wait_ge(state_ready, 1 + STEPS)
            for s in range(GROUPS + 4):
                if s < GROUPS:
                    g = s
                    if g >= 2:
                        pe.wait_ge(hid_ready, g - 1)
                    pe.matmul(bank[g % 2][:], ct, states[:, MAIN + g * GC:MAIN + (g + 1) * GC], start=True, stop=True
                              ).then_inc(c_done, 1)
                if 0 <= s - 1 < GROUPS:
                    g = s - 1
                    pe.wait_ge(hid_ready, g + 1)
                    if g >= 2:
                        pe.wait_ge(tanh_ready, g - 1)
                    pe.matmul(bank[2 + g % 2][:], wgt, hid[:, g % 2, :], start=True, stop=True).then_inc(wg_done, 1)
                if 0 <= s - 2 < GROUPS:
                    g = s - 2
                    pe.wait_ge(gated_ready, g + 1)
                    if g >= 2:
                        pe.wait_ge(attn_ready, g - 1)
                    for i in range(4):
                        mm = pe.matmul(bank[4 + g % 2][:, i * P:(i + 1) * P], gated[:, g % 2, i * P:(i + 1) * P], wot,
                                       start=True, stop=True)
                    mm.then_inc(wo_done, 1)
                if 0 <= s - 4 < GROUPS:
                    g = s - 4
                    if g >= 1:
                        pe.wait_ge(xffn_ready, g)
                    for i in range(4):
                        pe.wait_ge(rows_ready, 4 * g + i + 1)
                        mm = pe.transpose(bank[6][:, i * P:(i + 1) * P], rows[:, 4 * g + i, 0:P], ident)
                    mm.then_inc(rows_turned, 1)
                    pe.wait_ge(xffn_ready, g + 1)
                    for i in range(4):
                        t = 4 * g + i
                        mm = pe.matmul(bank[7][:, t * EXPERTS:(t + 1) * EXPERTS], x_ffn[:, t * P:(t + 1) * P], gate_sb[:],
                                       start=True, stop=True)
                    if g == GROUPS - 1:
                        mm.then_inc(logits_done, 1)

            def up(g):
                for i in range(IC):
                    n = g * IC + i
                    if n >= 2:
                        pe.wait_ge(gelu_done, n - 1)
                    pe.matmul(bank[n % 2][:], sw1_sb[:, i * P:(i + 1) * P], x_ffn[:, g * GC:(g + 1) * GC],
                              start=True, stop=True).then_inc(up_done, 1)

            def down(g):
                pe.wait_ge(gelu_done, (g + 1) * IC)
                if g >= 2:
                    pe.wait_ge(base_ready, g - 1)
                for t in range(4):
                    for i in range(IC):
                        mm = pe.matmul(bank[2 + g % 2][:, t * P:(t + 1) * P], act_sh[:, g % 2, i, t * P:(t + 1) * P],
                                       sw2_sb[:, i, :], start=(i == 0), stop=(i == IC - 1))
                mm.then_inc(down_done, 1)

            pe.wait_ge(sh_weights_in, 32)
            up(0)
            pe.wait_ge(onehot_ready, 1)
            pe.matmul(bank[4][:, 0:P], ones, onehot[:], start=True, stop=True)
            pe.matmul(bank[5][:, 0:P], cst[:, C_RANK:C_RANK + P], onehot[:], start=True, stop=True).then_inc(counts_done, 1)
            up(1)
            down(0)
            up(2)
            down(1)
            up(3)
            down(2)
            down(3)

            pe.wait_ge(weights_in, 48)
            pe.wait_ge(experts_ready, 1)
            pe.wait_ge(base_ready, GROUPS)

            def turn_block(k, u):
                pe.wait_ge(xblk_in[u], pair_count(k, u, 16))
                pe.transpose(bank[5][:, 0:P], xblk[:, u, :], ident).then_inc(blk_turned, 1)

            def step(k, u, static):
                live = lambda d: static is None or 0 <= static - d < BLOCKS
                if live(0):
                    e = pe.value_load(block_expert[0:1, bass.ds(k, 1)], min_val=0, max_val=EXPERTS - 1)
                    pe.wait_ge(xt_ready, k + 1)
                    if static is None or static >= 2:
                        pe.wait_ge(prod_ready, k - 1)
                    pe.matmul(bank[u][:], xblk_t[:, u, :], w1_sb[:, bass.ds(e * INNER, INNER)], start=True, stop=True
                              ).then_inc(h_done, 1)
                    pe.matmul(bank[2 + u][:], xblk_t[:, u, :], w3_sb[:, bass.ds(e * INNER, INNER)], start=True, stop=True
                              ).then_inc(h_done, 1)
                if live(-1):
                    turn_block(k + 1, 1 - u)
                if live(1):
                    pe.wait_ge(prod_ready, k)
                    if static is None or static >= 2:
                        pe.wait_ge(prodt_ready, k - 1)
                    for i in range(IC):
                        mm = pe.transpose(bank[4][:, i * P:(i + 1) * P], prod[:, 1 - u, i * P:(i + 1) * P], ident)
                    mm.then_inc(prod_turned, 1)
                if live(2):
                    e2 = pe.value_load(block_expert[0:1, bass.ds(k - 2, 1)], min_val=0, max_val=EXPERTS - 1)
                    pe.wait_ge(prodt_ready, k - 1)
                    if static is None or static >= 3:
                        pe.wait_ge(outb_ready, k - 2)
                    for i in range(IC):
                        mm = pe.matmul(bank[6][:, 0:P], prod_t[:, u, i * P:(i + 1) * P],
                                       w2_sb[:, bass.ds(e2 * INNER + i * P, P)], start=(i == 0), stop=(i == IC - 1))
                    mm.then_inc(y_done, 1)

            turn_block(0, 0)
            pipelined(pe, step, 2)

        @block.scalar
        def _(act):
            for g in range(GROUPS):
                act.wait_ge(norm_turned, g + 1)
                dst = x_in[:, 8 * g * XW:(8 * g + 8) * XW].rearrange("h (p k) -> h p k", k=XW)[:, :, PADC:XW]
                act.activation(dst, bank[g % 2][:].rearrange("h (p k) -> h p k", k=COLS), ACT.Copy).then_inc(x_ready, 1)
            for i in range(STEPS):
                act.wait_ge(pre_ready, i + 1)
                act.activation(states[:, (i + 1) * COLS:(i + 2) * COLS], bank[i % 2][:, 0:COLS], ACT.Tanh
                               ).then_inc(state_ready, 1)
            act.wait_ge(agree_ready, 1)
            ok = act.value_load(agree_i[0:1, 0:1], min_val=0, max_val=1)
            with act.If(ok == 0):
                with act.Fori(0, CHUNKS) as c:
                    for p in range(CHUNK):
                        act.wait_ge(seq_pre, c * CHUNK + (p + 1))
                        act.activation(piece[:, p, :], bank[p % 2][:, 0:BATCH], ACT.Tanh).then_inc(seq_state, 1)
                    act.wait_ge(seq_state, c * CHUNK + (CHUNK + 1))
                    act.activation(states[:, MAIN:].rearrange("h (p k) -> h p k", k=COLS)[:, :, bass.ds(c * BATCH, BATCH)],
                                   piece[:], ACT.Copy).then_inc(seq_kept, 1)
                    act.wait_ge(seq_kept, c + 1)
            act.wait_ge(bg_ready, 1)
            for s in range(GROUPS + 2):
                if s < GROUPS:
                    g = s
                    act.wait_ge(wg_done, g + 1)
                    if g >= 2:
                        act.wait_ge(gated_ready, g - 1)
                    act.activation(gate_t[:, g % 2, :], bank[2 + g % 2][:], ACT.Tanh, bias=half_bg[:, 0:1], scale=0.5
                                   ).then_inc(tanh_ready, 1)
                if s >= 2:
                    g = s - 2
                    act.wait_ge(rows_turned, g + 1)
                    act.activation(x_ffn[:, g * GC:(g + 1) * GC], bank[6][:], ACT.Copy).then_inc(xffn_ready, 1)
            for n in range(GROUPS * IC):
                g, i = divmod(n, IC)
                act.wait_ge(up_done, n + 1)
                if g >= 2:
                    act.wait_ge(down_done, g - 1)
                act.activation(act_sh[:, g % 2, i, :], bank[n % 2][:], ACT.Gelu).then_inc(gelu_done, 1)

            def step(k, u, static):
                if static is None or static < BLOCKS:
                    act.wait_ge(h_done, k * 2 + 1)
                    if static is None or static >= 2:
                        act.wait_ge(prod_ready, k - 1)
                    act.activation(silu[:, u, :], bank[u][:], ACT.Silu).then_inc(silu_ready, 1)
                if static is None or static >= 1:
                    act.wait_ge(prod_turned, k)
                    if static is None or static >= 3:
                        act.wait_ge(y_done, k - 2)
                    act.activation(prod_t[:, 1 - u, :], bank[4][:], ACT.Copy).then_inc(prodt_ready, 1)

            pipelined(act, step, 1)

        @block.vector
        def _(dve):
            n_step = [0]

            def then_wait(ins):
                n_step[0] += 1
                ins.then_inc(dve_step, 1)
                dve.wait_ge(dve_step, n_step[0])

            dve.memset(states[:, 0:COLS], 0.0)
            dve.memset(piece[:, CHUNK - 1, :], 0.0).then_inc(seq_state, 1)
            dve.memset(x_in[:].rearrange("h (p k) -> h p k", k=XW)[:, :, 0:PADC], 0.0).then_inc(pads_zero, 1)
            dve.memset(diff[:], 0.0).then_inc(state_ready, 1)
            dve.wait_ge(small_in, 80)
            dve.tensor_scalar(half_bg[:], bg_sb[:], 0.5, None, ALU.mult).then_inc(bg_ready, 1)

            def statistics(src, st, mv, ve, g, ready):
                for t in range(4 * g, 4 * g + 4):
                    ins = dve.bn_stats(st[:, t, :], src[:, t, :])
                then_wait(ins)
                for t in range(4 * g, 4 * g + 4):
                    ins = dve.bn_aggr(mv[:, t, :], st[:, t, :])
                then_wait(ins)
                ts = slice(4 * g, 4 * g + 4)
                dve.tensor_scalar(ve[:, ts], mv[:, ts, 1], EPS, None, ALU.add).then_inc(ready, 1)

            def normalise(dst, src, mv, rs, g, rs_ready, ready):
                dve.wait_ge(rs_ready, g + 1)
                for t in range(4 * g, 4 * g + 4):
                    dve.tensor_scalar(dst[:, t, 0:P], src[:, t, :], mv[:, t, 0:1], rs[:, t:t + 1],
                                      ALU.subtract, ALU.mult).then_inc(ready, 1)

            for g in range(GROUPS):
                dve.wait_ge(gathered[g], 64)
                statistics(emb_rows, stats, meanvar, vareps, g, var_ready)
            for g in range(GROUPS):
                normalise(norm_rows, emb_rows, meanvar, rstd, g, rstd_ready, norm_ready)

            dve.wait_ge(state_ready, 1 + STEPS)
            then_wait(dve.tensor_tensor(diff[:], states[:, MAIN - COLS + BATCH:MAIN],
                                        states[:, STEPS * COLS:(1 + STEPS) * COLS - BATCH], ALU.subtract))
            then_wait(dve.tensor_tensor(diff2[:], diff[:], diff[:], ALU.mult))
            then_wait(dve.tensor_scalar(close[:], diff2[:], TOL * TOL, None, ALU.is_le))
            dve.tensor_reduce(close_row[:], close[:], AX.X, ALU.min).then_inc(close_ready, 1)
            dve.wait_ge(close_turned, 1)
            then_wait(dve.tensor_reduce(agree[:], bank[2][0:1, 0:P], AX.X, ALU.min))
            dve.tensor_copy(agree_i[:], agree[:]).then_inc(agree_ready, 1)

            for s in range(GROUPS + 3):
                if s < GROUPS:
                    g = s
                    dve.wait_ge(c_done, g + 1)
                    if g >= 2:
                        dve.wait_ge(wg_done, g - 1)
                        dve.wait_ge(gated_ready, g - 1)
                    dve.tensor_copy(hid[:, g % 2, :], bank[g % 2][:]).then_inc(hid_ready, 1)
                if 0 <= s - 1 < GROUPS:
                    g = s - 1
                    dve.wait_ge(tanh_ready, g + 1)
                    dve.wait_ge(hid_ready, g + 1)
                    if g >= 2:
                        dve.wait_ge(wo_done, g - 1)
                    dve.scalar_tensor_tensor(out=gated[:, g % 2, :], in0=gate_t[:, g % 2, :], scalar=1.0,
                                             in1=hid[:, g % 2, :], op0=ALU.add, op1=ALU.mult).then_inc(gated_ready, 1)
                if 0 <= s - 2 < GROUPS:
                    g = s - 2
                    ts = slice(4 * g, 4 * g + 4)
                    dve.wait_ge(wo_done, g + 1)
                    dve.wait_ge(resid_ready, g + 1)
                    dve.scalar_tensor_tensor(out=attn_out[:, ts, :], in0=bank[4 + g % 2][:].rearrange("q (t d) -> q t d", t=4),
                                             scalar=0.5, in1=resid_bo[:, ts, :], op0=ALU.mult, op1=ALU.add
                                             ).then_inc(attn_ready, 1)
                    dve.wait_ge(attn_ready, g + 1)
                    statistics(attn_out, stats2, meanvar2, vareps2, g, var2_ready)
                if 0 <= s - 3 < GROUPS:
                    normalise(rows, attn_out, meanvar2, rstd2, s - 3, rstd2_ready, rows_ready)

            te = lambda ap: ap.rearrange("q (t e) -> q t e", e=EXPERTS)
            et = lambda ap: ap.rearrange("q (e t) -> q t e", e=EXPERTS)
            over = lambda ap: ap.unsqueeze(2).to_broadcast([P, TILES, EXPERTS])
            logits = bank[7][:, 0:ET]
            rev = cst[:, C_REV:C_REV + ET]
            dve.wait_ge(logits_done, 1)
            then_wait(dve.tensor_reduce(top[:], te(logits), AX.X, ALU.max))
            then_wait(dve.tensor_tensor(te(is_top[:]), te(logits), over(top[:]), ALU.is_ge))
            then_wait(dve.tensor_tensor(rev_top[:], is_top[:], rev, ALU.mult))
            then_wait(dve.tensor_reduce(first_rev[:], te(rev_top[:]), AX.X, ALU.max))
            dve.tensor_tensor(et(onehot[:]), te(rev), over(first_rev[:]), ALU.is_equal).then_inc(onehot_ready, 1)
            dve.wait_ge(counts_done, 1)
            dve.wait_ge(onehot_ready, 1)
            then_wait(dve.tensor_tensor_scan(upto[:], cst[:, C_CARRY:C_CARRY + ET], bank[4][:, 0:ET], 0.0,
                                             ALU.mult, ALU.add))
            then_wait(dve.tensor_tensor(place[:], bank[5][:, 0:ET], upto[:], ALU.add))
            counts = upto[:].rearrange("q (e t) -> q e t", e=EXPERTS)[:, :, TILES - 1]
            then_wait(dve.tensor_scalar(blocks_i0[:], counts, float(P - 1), None, ALU.add))
            then_wait(dve.tensor_scalar(blocks_i[:], blocks_i0[:], 7, None, ALU.logical_shift_right))
            then_wait(dve.tensor_tensor_scan(blocks_end[:], cst[:, C_ONES:C_ONES + EXPERTS], blocks_i[:], 0.0,
                                             ALU.mult, ALU.add))
            then_wait(dve.tensor_tensor(blocks_start[:], blocks_end[:], blocks_i[:], ALU.subtract))
            e_t = lambda ap: ap.rearrange("q (e t) -> q e t", e=EXPERTS)
            then_wait(dve.scalar_tensor_tensor(out=e_t(place_all[:]),
                                               in0=blocks_start[:].unsqueeze(2).to_broadcast([P, EXPERTS, TILES]),
                                               scalar=float(P), in1=e_t(place[:]), op0=ALU.mult, op1=ALU.add))
            then_wait(dve.tensor_tensor(place_own[:], place_all[:], onehot[:], ALU.mult))
            then_wait(dve.tensor_reduce(slot_f[:], et(place_own[:]), AX.X, ALU.add))
            dve.tensor_copy(slot_i[:], slot_f[:]).then_inc(slots_ready, 1)
            k_e = lambda ap: ap.rearrange("q (k e) -> q k e", e=EXPERTS)
            then_wait(dve.tensor_tensor(k_e(past[:]), k_e(cst[0:1, C_BLOCK:C_BLOCK + BLOCKS * EXPERTS]),
                                        blocks_end[0:1, :].unsqueeze(1).to_broadcast([1, BLOCKS, EXPERTS]), ALU.is_ge))
            then_wait(dve.tensor_reduce(block_expert_f[:], k_e(past[:]), AX.X, ALU.add))
            dve.tensor_scalar(block_expert[:], block_expert_f[:], float(EXPERTS - 1), None, ALU.min
                              ).then_inc(experts_ready, 1)

            for g in range(GROUPS):
                ts = slice(4 * g, 4 * g + 4)
                dve.wait_ge(down_done, g + 1)
                dve.tensor_tensor(base[:, ts, :], bank[2 + g % 2][:].rearrange("q (t d) -> q t d", t=4),
                                  attn_out[:, ts, :], ALU.add).then_inc(base_ready, 1)

            def take_turned(k, u):
                dve.wait_ge(blk_turned, k + 1)
                dve.tensor_copy(xblk_t[:, u, :], bank[5][:, 0:P]).then_inc(xt_ready, 1)

            def step(k, u, static):
                live = lambda d: static is None or 0 <= static - d < BLOCKS
                if live(-1):
                    take_turned(k + 1, 1 - u)
                if live(0):
                    dve.wait_ge(silu_ready, k + 1)
                    dve.wait_ge(h_done, k * 2 + 2)
                    if static is None or static >= 2:
                        dve.wait_ge(prod_turned, k - 1)
                    dve.tensor_tensor(prod[:, u, :], bank[2 + u][:], silu[:, u, :], ALU.mult).then_inc(prod_ready, 1)
                if live(2):
                    dve.wait_ge(y_done, k - 1)
                    dve.wait_ge(res_in[u], pair_count(k - 2, u, 16))
                    if static is None or static >= 4:
                        dve.wait_ge(out_stored[u], pair_count(k - 4, u, 16))
                    dve.tensor_tensor(out_blk[u][:], bank[6][:, 0:P], res_blk[u][:], ALU.add).then_inc(outb_ready, 1)

            take_turned(0, 0)
            pipelined(dve, step, 2)


_ARGS = ("tok", "ids", "consts", "emb", "sq", "bg", "bo", "gate", "w1", "w3", "w2", "sw1", "sw2")


def kernel(x, L0_tok_W, L0_attn_A, L0_attn_B, L0_attn_C, L0_attn_Wg, L0_attn_bg, L0_attn_Wo, L0_attn_bo,
           L0_ffn_gate_w, L0_ffn_w1, L0_ffn_w2, L0_ffn_w3, L0_ffn_sw1, L0_ffn_sw2):
    import concourse.bacc as bacc
    from concourse.bass_utils import run_bass_kernel_spmd

    row = np.ascontiguousarray
    tok = np.asarray(x).reshape(BATCH, CHUNKS, TILES, 2).transpose(3, 1, 0, 2).reshape(P, TILES)
    arrays = {
        "tok": row(tok),
        "ids": row_ids(),
        "consts": shape_constants(),
        "emb": row(np.asarray(L0_tok_W).T),
        "sq": row(np.stack([np.asarray(w).T for w in (L0_attn_A, L0_attn_B, L0_attn_C, L0_attn_Wg, L0_attn_Wo)], 1)),
        "bg": row(np.asarray(L0_attn_bg).reshape(P, 1)),
        "bo": row(np.asarray(L0_attn_bo).reshape(1, P)),
        "gate": row(np.asarray(L0_ffn_gate_w).T),
        "w1": row(np.asarray(L0_ffn_w1).transpose(2, 0, 1).reshape(P, EXPERTS * INNER)),
        "w3": row(np.asarray(L0_ffn_w3).transpose(2, 0, 1).reshape(P, EXPERTS * INNER)),
        "w2": row(np.asarray(L0_ffn_w2).reshape(EXPERTS, P, IC, P).transpose(3, 0, 2, 1).reshape(P, EXPERTS * INNER)),
        "sw1": row(np.asarray(L0_ffn_sw1).T),
        "sw2": row(np.asarray(L0_ffn_sw2).reshape(P, IC, P).transpose(2, 1, 0)),
    }
    nc = bacc.Bacc("TRN2", target_bir_lowering=False, num_devices=1)
    aps = [nc.dram_tensor(n, arrays[n].shape, mybir.dt.from_np(arrays[n].dtype), kind="ExternalInput").ap()
           for n in _ARGS]
    out = nc.dram_tensor("out", (BATCH * SEQ, P), F32, kind="ExternalOutput").ap()
    dispatch = nc.dram_tensor("dispatch", (BLOCKS * P, ROW), F32).ap()
    resid = nc.dram_tensor("resid", (TILES * P, P), F32).ap()
    build(nc, *aps, out, dispatch, resid)
    got = run_bass_kernel_spmd(nc, [arrays], core_ids=[0])
    return got.results[0]["out"].reshape(BATCH, SEQ, P)
```

```python
from contextlib import ExitStack

import numpy as np
import concourse.bass as bass
from concourse import mybir

P = 128
BATCH, SEQ = 4, 512
EXPERTS, INNER = 8, 512
CHUNK = 32
CHUNKS = SEQ // CHUNK
WARM = 40
MEET = 5
COLS = CHUNKS * BATCH
PADC = 2 * BATCH
XW = COLS + PADC
STEPS = WARM + CHUNK
MAIN = (1 + WARM) * COLS
TILES = BATCH * SEQ // P
GROUPS = TILES // 4
GC = 4 * P
PAIRS = TILES // 2
PC = 2 * P
MAX_STEP = 40
HIGH_STEP = MAX_STEP + 6
FIRST_TILE = -WARM % CHUNK // 2
IC = INNER // P
QUARTERS = 4
GELUS = 8
WEIGHTS = 6
BLOCKS = TILES + EXPERTS - 1
ROW = 2 * P + 4
NO_ROW = 4096
RING = 4
X_SCALE = 2.0 ** 8
EPS = 1e-5
TOL = 2.0 ** -18

F32 = mybir.dt.float32
I32 = mybir.dt.int32
F16 = mybir.dt.float16
ALU = mybir.AluOpType
ACT = mybir.ActivationFunctionType
AX = mybir.AxisListType

C_IDENT, C_RANK, C_ONES, C_REV, C_CARRY, C_BLOCK, C_EPS, C_POW = 0, 128, 256, 384, 512, 640, 824, 840
C_END = 856


def shape_constants():
    c = np.zeros((P, C_END), np.float32)
    j = np.arange(P)
    c[:, C_IDENT:C_IDENT + P] = np.eye(P)
    c[:, C_RANK:C_RANK + P] = -(j[:, None] >= j[None, :]).astype(np.float32)
    c[:, C_ONES:C_ONES + P] = 1.0
    c[:, C_REV:C_REV + P] = np.tile(EXPERTS - np.arange(EXPERTS), TILES)
    c[:, C_CARRY:C_CARRY + P] = np.tile(np.arange(TILES) > 0, EXPERTS)
    c[:, C_BLOCK:C_BLOCK + BLOCKS * EXPERTS] = np.repeat(np.arange(BLOCKS), EXPERTS)
    c[:, C_EPS:C_EPS + TILES] = EPS
    c[:, C_POW:C_POW + TILES] = -0.5
    return c


def row_ids():
    q, t = np.arange(P)[:, None], np.arange(TILES)[None, :]
    pos = (q // BATCH % CHUNKS) * CHUNK + 2 * t + q // COLS
    return np.stack([(q % BATCH) * SEQ + pos, t * P + q], -1).astype(np.int32)


def build(nc, tok, ids, consts, emb, sq, bg, bo, gate, w1, w3, w2, sw1, sw2, out, dispatch, resid):
    with ExitStack() as ctx:
        def sb(name, shape, dt=F32):
            return ctx.enter_context(nc.sbuf_tensor(name, shape, dt))

        def sem(name):
            return ctx.enter_context(nc.semaphore(name))

        bank = [ctx.enter_context(nc.psum_tensor(f"bank{i}", [P, 512], F32)) for i in range(8)]

        tok_sb = sb("tok_sb", [P, TILES], I32)
        cst = sb("cst", [P, C_END])
        sq_sb = sb("sq_sb", [P, 6, P])
        bg_sb = sb("bg_sb", [P, 1])
        half_bg = sb("half_bg", [P, 1])
        bo_sb = sb("bo_sb", [P, P])
        gate_sb = sb("gate_sb", [P, EXPERTS])
        w1_hl, w3_hl = (sb(n, [P, 2, EXPERTS * INNER], F16) for n in ("w1_hl", "w3_hl"))
        w2_hl = sb("w2_hl", [P, EXPERTS * IC, 2, P], F16)
        sw1_hl, sw2_hl = (sb(n, [P, 2, INNER], F16) for n in ("sw1_hl", "sw2_hl"))
        gate_hl = sb("gate_hl", [P, 2, EXPERTS], F16)
        part_max = sb("part_max", [P, 3, QUARTERS])
        max_rows = sb("max_rows", [P, WEIGHTS])
        max_col = sb("max_col", [WEIGHTS, 1])
        max_diag = sb("max_diag", [WEIGHTS, WEIGHTS])
        max_all = sb("max_all", [P, WEIGHTS])
        max_exp, max_exp_in = (sb(n, [P, WEIGHTS], I32) for n in ("max_exp", "max_exp_in"))
        scale_i, unscale_i = (sb(n, [P, WEIGHTS], I32) for n in ("scale_i", "unscale_i"))
        factor = sb("factor", [P, 6])
        inv_w1w3, inv_w1w3w2, inv_sw = (sb(n, [P, 1]) for n in ("inv_w1w3", "inv_w1w3w2", "inv_sw"))
        ident16 = sb("ident16", [P, P], F16)
        w1_sb = sb("w1_sb", [P, EXPERTS * INNER])
        w3_sb = sb("w3_sb", [P, EXPERTS * INNER])
        w2_sb = sb("w2_sb", [P, EXPERTS * INNER])
        sw1_sb = sb("sw1_sb", [P, INNER])
        sw2_sb = sb("sw2_sb", [P, INNER])
        ident = cst[:, C_IDENT:C_IDENT + P]
        ones = cst[:, C_ONES:C_ONES + P]
        at, bt, ct, wgt, wot, c_nat = (sq_sb[:, i, :] for i in range(6))

        emb_rows = sb("emb_rows", [P, TILES, P])
        stats = sb("stats", [P, TILES, 6])
        meanvar = sb("meanvar", [P, TILES, 2])
        vareps = sb("vareps", [P, TILES])
        rstd = sb("rstd", [P, TILES])
        norm_rows = sb("norm_rows", [P, 4, P])
        x_in = sb("x_in", [P, CHUNK * XW])

        states = sb("states", [P, (1 + STEPS) * COLS])
        piece = sb("piece", [P, CHUNK, BATCH])
        diff = sb("diff", [P, COLS - BATCH])
        diff2 = sb("diff2", [P, COLS - BATCH])
        close = sb("close", [P, COLS - BATCH])
        close_row = sb("close_row", [P, 1])
        agree = sb("agree", [1, 1])
        agree_i = sb("agree_i", [1, 1], I32)

        wgc = sb("wgc", [P, P])
        gate_t = sb("gate_t", [P, 2, PC])
        gated = sb("gated", [P, 2, PC])
        attn_out = sb("attn_out", [P, TILES, P])
        stats2 = sb("stats2", [P, TILES, 6])
        meanvar2 = sb("meanvar2", [P, TILES, 2])
        vareps2 = sb("vareps2", [P, TILES])
        rstd2 = sb("rstd2", [P, TILES])
        norm2 = sb("norm2", [P, 4, P])
        rows = sb("rows", [P, TILES, ROW], F16)
        x_ffn = sb("x_ffn", [P, 2, TILES * P], F16)

        ET = EXPERTS * TILES
        logits = sb("logits", [P, ET])
        top = sb("top", [P, TILES])
        is_top = sb("is_top", [P, ET])
        rev_top = sb("rev_top", [P, ET])
        first_rev = sb("first_rev", [P, TILES])
        onehot = sb("onehot", [P, ET])
        upto = sb("upto", [P, ET])
        place = sb("place", [P, ET])
        place_all = sb("place_all", [P, ET])
        place_own = sb("place_own", [P, ET])
        blocks_i0 = sb("blocks_i0", [P, EXPERTS], I32)
        blocks_i = sb("blocks_i", [P, EXPERTS], I32)
        blocks_end = sb("blocks_end", [P, EXPERTS])
        blocks_start = sb("blocks_start", [P, EXPERTS])
        slot_f = sb("slot_f", [P, TILES])
        slot_i = sb("slot_i", [P, TILES], I32)
        past = sb("past", [1, BLOCKS * EXPERTS])
        block_expert_f = sb("block_expert_f", [1, BLOCKS])
        block_expert = sb("block_expert", [1, BLOCKS], I32)
        fill = sb("fill", [P, ROW], F16)
        ids_all = sb("ids_all", [P, BLOCKS, 4], F16)

        gelu = w1_sb[:].rearrange("i (n j) -> i n j", n=GELUS)
        act_hi, act_lo = (w[:, 4 * GC:8 * GC].bitcast(F16).rearrange("i (g n j) -> i g n j", g=2, n=IC)
                          for w in (w2_sb, w3_sb))

        xblk = sb("xblk", [P, RING, 2 * P], F16)
        xblk_t = sb("xblk_t", [P, 2, 2 * P], F16)
        silu, prod = (w3_sb[:, i * 2 * INNER:(i + 1) * 2 * INNER].rearrange("i (u j) -> i u j", u=2) for i in range(2))
        out_part = sb("out_part", [P, 2, P])
        prod_hi, prod_lo = (sb(n, [P, 2, INNER], F16) for n in ("prod_hi", "prod_lo"))
        idb = [sb(f"idb{i}", [P, 2], I32) for i in range(RING)]
        res_blk = [sb(f"res_blk{i}", [P, P]) for i in range(RING)]
        out_blk = [sb(f"out_blk{i}", [P, P]) for i in range(RING)]

        tok_in, small_in = sem("tok_in"), sem("small_in")
        w_in = [sem(f"w_in{j}") for j in range(3 * QUARTERS)]
        max_ready, max_turned, diag_ready, max_spread, scales_ready, ident16_ready = (
            sem(n) for n in ("max_ready", "max_turned", "diag_ready", "max_spread", "scales_ready", "ident16_ready"))
        w_high, sh_split, w_split = sem("w_high"), sem("sh_split"), sem("w_split")
        sh_weights_in = sem("sh_weights_in")
        ids_in, filled, fill_stored = sem("ids_in"), sem("filled"), sem("fill_stored")
        gathered = [sem(f"gathered{n}") for n in range(PAIRS)]
        dve_step, pool_step = sem("dve_step"), sem("pool_step")
        var_ready, rstd_ready, norm_ready = sem("var_ready"), sem("rstd_ready"), sem("norm_ready")
        norm_turned, x_ready, pads_zero = sem("norm_turned"), sem("x_ready"), sem("pads_zero")
        pre_ready, state_ready = sem("pre_ready"), sem("state_ready")
        close_ready, close_turned, agree_ready = sem("close_ready"), sem("close_turned"), sem("agree_ready")
        seq_pre, seq_state, seq_kept = sem("seq_pre"), sem("seq_state"), sem("seq_kept")
        bg_ready, resid_ready = sem("bg_ready"), sem("resid_ready")
        wgc_done, wgc_ready, c_done, wg_done, tanh_ready, gated_ready, wo_done, attn_ready = (
            sem(n) for n in ("wgc_done", "wgc_ready", "c_done", "wg_done", "tanh_ready", "gated_ready", "wo_done",
                             "attn_ready"))
        var2_ready, rstd2_ready, rows_ready, rows_turned, xffn_ready, logits_done = (
            sem(n) for n in ("var2_ready", "rstd2_ready", "rows_ready", "rows_turned", "xffn_ready", "logits_done"))
        norm2_ready, rows_high = sem("norm2_ready"), sem("rows_high")
        onehot_ready, counts_done, slots_ready, experts_ready = (
            sem(n) for n in ("onehot_ready", "counts_done", "slots_ready", "experts_ready"))
        dispatched = sem("dispatched")
        up_done, gelu_done, act_high, down_done, base_ready, base_stored = (
            sem(n) for n in ("up_done", "gelu_done", "act_high", "down_done", "base_ready", "base_stored"))
        act_low = sem("act_low")
        all_ids_in = sem("all_ids_in")
        xblk_in = [sem(f"xblk_in{i}") for i in range(RING)]
        res_in = [sem(f"res_in{i}") for i in range(RING)]
        out_stored = [sem(f"out_stored{i}") for i in range(RING)]
        id_copied, blk_turned, xt_ready, h_done, silu_ready, prod_ready, prod_turned, prod_high, prod_low, y_done, part_ready, outb_ready = (
            sem(n) for n in ("id_copied", "blk_turned", "xt_ready", "h_done", "silu_ready", "prod_ready",
                             "prod_turned", "prod_high", "prod_low", "y_done", "part_ready", "outb_ready"))
        res_zero, first_id_copied = sem("res_zero"), sem("first_id_copied")

        block = ctx.enter_context(nc.Block())

        def pipelined(eng, body, lag):
            lo = RING
            hi = lo + (BLOCKS - lo) // RING * RING
            for k in range(lo):
                body(k, k % RING, k)
            with eng.Fori(0, (hi - lo) // RING) as m:
                for v in range(RING):
                    body(m * RING + (lo + v), v, None)
            for k in range(hi, BLOCKS + lag):
                body(k, k % RING, k)

        def pair_tiles(n):
            t = (FIRST_TILE + 2 * n) % TILES
            return (t, t + 1)

        def quarter(j):
            width = EXPERTS * INNER // QUARTERS
            return slice(j % QUARTERS * width, (j % QUARTERS + 1) * width)

        def ts4(n):
            return slice(n % 2 * 2, n % 2 * 2 + 2)

        def ring_count(k, v):
            return (k - v) * (16 // RING) + 16

        scale, unscale = scale_i[:].bitcast(F32), unscale_i[:].bitcast(F32)
        silu_in, prod_scale, y_unscale, gelu_in, act_scale, base_unscale = (factor[:, i:i + 1] for i in range(6))

        @block.sync
        def _(sp):
            sp.dma_start(tok_sb[:], tok).then_inc(tok_in, 16)
            sp.dma_start(cst[:], consts).then_inc(small_in, 16)
            sp.dma_start(sq_sb[:], sq).then_inc(small_in, 16)
            sp.dma_start(bg_sb[:], bg).then_inc(small_in, 16)
            sp.dma_start(bo_sb[:], bo.to_broadcast([P, P])).then_inc(small_in, 16)
            sp.dma_start(gate_sb[:], gate).then_inc(small_in, 16)
            sp.dma_start(rows[:].bitcast(I32)[:, :, P:P + 2], ids).then_inc(ids_in, 16)
            sp.wait_ge(gathered[0], 32)
            sp.dma_start(sw1_sb[:], sw1).then_inc(sh_weights_in, 16)
            sp.dma_start(sw2_sb[:], sw2).then_inc(sh_weights_in, 16)
            for j in range(3 * QUARTERS):
                if 1 + j < PAIRS:
                    sp.wait_ge(gathered[1 + j], 32)
                w_sb, w = ((w1_sb, w1), (w3_sb, w3), (w2_sb, w2))[j // QUARTERS]
                sp.dma_start(w_sb[:, quarter(j)], w[:, quarter(j)]).then_inc(w_in[j], 16)
            sp.wait_ge(filled, 2)
            sp.dma_start(dispatch.rearrange("(k p) c -> p k c", p=P),
                         fill[:].unsqueeze(1).to_broadcast([P, BLOCKS, ROW])).then_inc(fill_stored, 16)
            sp.wait_ge(dispatched, 16 * TILES)
            sp.dma_start(ids_all[:], dispatch.rearrange("(k p) c -> p k c", p=P)[:, :, 2 * P:ROW]).then_inc(all_ids_in, 16)

            def load_block(k, v, static):
                if static is None or static >= RING:
                    sp.wait_ge(blk_turned, k - (RING - 1))
                sp.dma_start(xblk[:, v, :], dispatch[bass.ds(k * P, P), 0:2 * P]).then_inc(xblk_in[v], 16)

            for k in range(RING):
                load_block(k, k, k)
            for g in range(GROUPS):
                sp.wait_ge(base_ready, g + 1)
                sp.dma_start(resid.rearrange("(t p) d -> p t d", p=P)[:, 4 * g:4 * g + 4, :],
                             attn_out[:, 4 * g:4 * g + 4, :]).then_inc(base_stored, 16)
            with sp.Fori(0, BLOCKS // RING - 1) as m:
                for v in range(RING):
                    load_block(m * RING + (RING + v), v, None)
            for k in range(BLOCKS // RING * RING, BLOCKS):
                load_block(k, k % RING, k)
            for v in range(RING):
                sp.wait_ge(out_stored[v], 16 * len(range(v, BLOCKS, RING)))

        @block.gpsimd
        def _(pool):
            pool.memset(fill[:, 0:2 * P], 0.0).then_inc(filled, 1)
            pool.memset(fill[:].bitcast(I32)[:, P:P + 2], NO_ROW).then_inc(filled, 1)
            pool.wait_ge(tok_in, 16)
            for n in range(PAIRS + 2):
                if n < PAIRS:
                    for t in pair_tiles(n):
                        pool.indirect_dma_start(out=emb_rows[:, t, :], out_offset=None, in_=emb,
                                                in_offset=bass.IndirectOffsetOnAxis(ap=tok_sb[:, t:t + 1], axis=0),
                                                ).then_inc(gathered[n], 16)
                if n >= 2:
                    t0 = pair_tiles(n - 2)[0]
                    if n == 2:
                        pool.wait_ge(small_in, 80)
                    pool.wait_ge(var_ready, n - 1)
                    pool.tensor_tensor(rstd[:, t0:t0 + 2], vareps[:, t0:t0 + 2], cst[:, C_POW:C_POW + 2], ALU.pow
                                       ).then_inc(rstd_ready, 1)
            pool.wait_ge(norm_ready, TILES)
            for g in range(GROUPS):
                ts = slice(4 * g, 4 * g + 4)
                pool.tensor_tensor(emb_rows[:, ts, :], emb_rows[:, ts, :],
                                   bo_sb[:].unsqueeze(1).to_broadcast([P, 4, P]), ALU.add).then_inc(resid_ready, 1)
            for i in range(RING):
                pool.memset(res_blk[i][:], 0.0).then_inc(res_zero, 1)
            for s in range(PAIRS + 1):
                if s < PAIRS:
                    ts = slice(2 * s, 2 * s + 2)
                    pool.wait_ge(var2_ready, s + 1)
                    pool.tensor_tensor(rstd2[:, ts], vareps2[:, ts], cst[:, C_POW:C_POW + 2], ALU.pow
                                       ).then_inc(rstd2_ready, 1)
                if s >= 1:
                    n = s - 1
                    ts = slice(2 * n, 2 * n + 2)
                    pool.wait_ge(rows_high, n + 1)
                    pool.tensor_tensor(rows[:, ts, P:2 * P], norm2[:, ts4(n), :], rows[:, ts, 0:P], ALU.subtract
                                       ).then_inc(rows_ready, 1)
            pool.wait_ge(fill_stored, 16)
            pool.wait_ge(ids_in, 16)
            pool.wait_ge(rows_ready, PAIRS)
            pool.wait_ge(slots_ready, 1)
            for t in range(TILES):
                pool.indirect_dma_start(out=dispatch, out_offset=bass.IndirectOffsetOnAxis(ap=slot_i[:, t:t + 1], axis=0),
                                        in_=rows[:, t, :], in_offset=None).then_inc(dispatched, 16)
            pool.wait_ge(all_ids_in, 16)
            pool.wait_ge(res_zero, RING)
            last_row = pool.to_reg(TILES * P - 1)

            def step(k, v, static):
                if static is None:
                    pool.wait_ge(id_copied, k - 1)
                if static is None or static < BLOCKS:
                    if static is None or static >= RING:
                        pool.wait_ge(out_stored[v], ring_count(k - RING, v))
                    pool.tensor_copy(idb[v][:], ids_all[:].bitcast(I32).rearrange("p k c -> p (k c)")[:, bass.ds(k * 2, 2)]
                                     ).then_inc(first_id_copied if static == 0 else id_copied, 1)
                    pool.wait_ge(base_stored, 16 * GROUPS)
                    if static == 0:
                        pool.wait_ge(first_id_copied, 1)
                    else:
                        pool.wait_ge(id_copied, k)
                    pool.indirect_dma_start(out=res_blk[v][:], out_offset=None, in_=resid,
                                            in_offset=bass.IndirectOffsetOnAxis(ap=idb[v][:, 1:2], axis=0),
                                            bounds_check=last_row, oob_is_err=False).then_inc(res_in[v], 16)
                if static is None or 2 <= static:
                    w = (v - 2) % RING
                    pool.wait_ge(all_ids_in, 16)
                    pool.wait_ge(outb_ready, k - 1)
                    pool.indirect_dma_start(out=out, out_offset=bass.IndirectOffsetOnAxis(ap=idb[w][:, 0:1], axis=0),
                                            in_=out_blk[w][:], in_offset=None,
                                            bounds_check=last_row, oob_is_err=False).then_inc(out_stored[w], 16)

            pipelined(pool, step, 2)

        @block.tensor
        def _(pe):
            pe.wait_ge(small_in, 80)
            pe.matmul(bank[4][:, 0:P], c_nat, wgt, start=True, stop=True).then_inc(wgc_done, 1)

            def turn_pair(n):
                if n >= 2:
                    pe.wait_ge(x_ready, n - 1)
                for i in range(2):
                    pe.wait_ge(norm_ready, 2 * n + i + 1)
                    mm = pe.transpose(bank[2 + n % 2][:, i * P:(i + 1) * P], norm_rows[:, n % 2 * 2 + i, :], ident)
                mm.then_inc(norm_turned, 1)

            turn_pair(0)
            pe.wait_ge(pads_zero, 1)
            for i in range(STEPS):
                if i < CHUNK and i % 4 == 0:
                    pe.wait_ge(x_ready, i // 4 + 1)
                shift = -((i - WARM) // CHUNK)
                p = (i - WARM) % CHUNK
                x_at = p * XW + PADC - shift * BATCH
                pre = bank[i % 2][:, 0:COLS]
                pe.matmul(pre, bt, x_in[:, x_at:x_at + COLS], start=True, stop=False)
                pe.wait_ge(state_ready, i + 1)
                pe.matmul(pre, at, states[:, i * COLS:(i + 1) * COLS], start=False, stop=True).then_inc(pre_ready, 1)
                if i < CHUNK - 4 and i % 4 == 1:
                    turn_pair(i // 4 + 1)
                if i == MAX_STEP:
                    pe.wait_ge(max_ready, 1)
                    pe.transpose(bank[5][0:WEIGHTS, 0:P], max_rows[:], ident).then_inc(max_turned, 1)
                if i == MAX_STEP + 2:
                    pe.wait_ge(diag_ready, 1)
                    pe.matmul(bank[6][:, 0:WEIGHTS], ones[0:WEIGHTS, :], max_diag[:], start=True, stop=True
                              ).then_inc(max_spread, 1)
                if i == STEPS - 3:
                    pe.wait_ge(close_ready, 1)
                    pe.transpose(bank[2][0:1, 0:P], close_row[:, 0:1], ident).then_inc(close_turned, 1)
                if i == STEPS - 2:
                    pe.wait_ge(agree_ready, 1)
                    ok = pe.value_load(agree_i[0:1, 0:1], min_val=0, max_val=1)

            with pe.If(ok == 0):
                pe.wait_ge(state_ready, 1 + STEPS)
                with pe.Fori(0, CHUNKS) as c:
                    for p in range(CHUNK):
                        pre = bank[p % 2][:, 0:BATCH]
                        pe.matmul(pre, bt, x_in[:, bass.ds(c * BATCH + (p * XW + PADC), BATCH)], start=True, stop=False)
                        pe.wait_ge(seq_state, c * CHUNK + (p + 1))
                        pe.matmul(pre, at, piece[:, (p - 1) % CHUNK, :], start=False, stop=True).then_inc(seq_pre, 1)
                pe.wait_ge(seq_kept, CHUNKS)

            pe.wait_ge(wgc_ready, 1)
            pe.wait_ge(ident16_ready, 1)
            pe.wait_ge(sh_split, 3)
            pe.wait_ge(state_ready, 1 + STEPS)
            for s in range(PAIRS + 4):
                if s < PAIRS:
                    n = s
                    kept = states[:, MAIN + n * PC:MAIN + (n + 1) * PC]
                    if n >= 2:
                        pe.wait_ge(tanh_ready, n - 1)
                    pe.matmul(bank[2 + n % 2][:, 0:PC], wgc[:], kept, start=True, stop=True).then_inc(wg_done, 1)
                    if n >= 2:
                        pe.wait_ge(gated_ready, n - 1)
                    pe.matmul(bank[n % 2][:, 0:PC], ct, kept, start=True, stop=True).then_inc(c_done, 1)
                if 0 <= s - 1 < PAIRS:
                    n = s - 1
                    pe.wait_ge(gated_ready, n + 1)
                    if n >= 2:
                        pe.wait_ge(attn_ready, n - 1)
                    for i in range(2):
                        mm = pe.matmul(bank[4 + n % 2][:, i * P:(i + 1) * P], gated[:, n % 2, i * P:(i + 1) * P], wot,
                                       start=True, stop=True)
                    mm.then_inc(wo_done, 1)
                if 0 <= s - 3 < PAIRS:
                    n = s - 3
                    if n >= 1:
                        pe.wait_ge(xffn_ready, n)
                    pe.wait_ge(rows_ready, n + 1)
                    for h in range(2):
                        for i in range(2):
                            mm = pe.transpose(bank[6][:].bitcast(F16)[:, (2 * h + i) * P:(2 * h + i + 1) * P],
                                              rows[:, 2 * n + i, h * P:(h + 1) * P], ident16[:])
                    mm.then_inc(rows_turned, 1)
                if 0 <= s - 4 < PAIRS:
                    n = s - 4
                    pe.wait_ge(xffn_ready, n + 1)
                    for t in range(2 * n, 2 * n + 2):
                        for h in range(2):
                            mm = pe.matmul(bank[7][:, t * 2 * EXPERTS:(t + 1) * 2 * EXPERTS],
                                           x_ffn[:, h, t * P:(t + 1) * P], gate_hl[:].rearrange("d h e -> d (h e)"),
                                           start=(h == 0), stop=(h == 1))
                    if n == PAIRS - 1:
                        mm.then_inc(logits_done, 1)

            halves = ((0, 0), (0, 1), (1, 0))

            def up(g):
                for i in range(IC):
                    n = g * IC + i
                    if n >= 2:
                        pe.wait_ge(gelu_done, n - 1)
                    for j, (a, b) in enumerate(halves):
                        mm = pe.matmul(bank[n % 2][:], sw1_hl[:, a, i * P:(i + 1) * P], x_ffn[:, b, g * GC:(g + 1) * GC],
                                       start=(j == 0), stop=(j == 2))
                    mm.then_inc(up_done, 1)

            def down(g):
                pe.wait_ge(act_low, (g + 1) * IC)
                if g >= 2:
                    pe.wait_ge(base_ready, g - 1)
                for t in range(4):
                    for i in range(IC):
                        for j, (a, b) in enumerate(halves):
                            mm = pe.matmul(bank[2 + g % 2][:, t * P:(t + 1) * P],
                                           (act_hi, act_lo)[a][:, g % 2, i, t * P:(t + 1) * P],
                                           sw2_hl[:, b, i * P:(i + 1) * P],
                                           start=(i == 0 and j == 0), stop=(i == IC - 1 and j == 2))
                mm.then_inc(down_done, 1)

            up(0)
            pe.wait_ge(onehot_ready, 1)
            pe.matmul(bank[4][:, 0:P], ones, onehot[:], start=True, stop=True)
            pe.matmul(bank[5][:, 0:P], cst[:, C_RANK:C_RANK + P], onehot[:], start=True, stop=True).then_inc(counts_done, 1)
            up(1)
            for g in range(2, GROUPS):
                down(g - 2)
                up(g)
            down(GROUPS - 2)
            down(GROUPS - 1)

            pe.wait_ge(w_split, 3)
            pe.wait_ge(experts_ready, 1)
            pe.wait_ge(base_ready, GROUPS)

            def turn_block(k, v, static):
                pe.wait_ge(xblk_in[v], ring_count(k, v))
                if static is None or static >= 1:
                    pe.wait_ge(xt_ready, k)
                for h in range(2):
                    mm = pe.transpose(bank[5][:].bitcast(F16)[:, h * P:(h + 1) * P], xblk[:, v, h * P:(h + 1) * P],
                                      ident16[:])
                mm.then_inc(blk_turned, 1)

            expert_of = [pe.alloc_register(f"expert_of{v}") for v in range(RING)]

            def load_expert(k, v):
                pe.reg_load(expert_of[v], block_expert[0:1, bass.ds(k, 1)])

            def step(k, v, static):
                live = lambda d: static is None or 0 <= static - d < BLOCKS
                u = v % 2
                if live(0):
                    e = pe.snap(expert_of[v], min_val=0, max_val=EXPERTS - 1)
                    pe.wait_ge(xt_ready, k + 1)
                    if static is None or static >= 2:
                        pe.wait_ge(prod_ready, k - 1)
                    for w_hl, hb in ((w1_hl, bank[u]), (w3_hl, bank[2 + u])):
                        w = w_hl[:].rearrange("d h c -> d (h c)")
                        for j, (a, b) in enumerate(halves):
                            mm = pe.matmul(hb[:], xblk_t[:, u, b * P:(b + 1) * P],
                                           w[:, bass.ds(e * INNER + a * EXPERTS * INNER, INNER)],
                                           start=(j == 0), stop=(j == 2))
                        mm.then_inc(h_done, 1)
                if live(-1):
                    load_expert(k + 1, (v + 1) % RING)
                    turn_block(k + 1, (v + 1) % RING, None if static is None else static + 1)
                if live(2):
                    e2 = pe.snap(expert_of[(v - 2) % RING], min_val=0, max_val=EXPERTS - 1)
                    pe.wait_ge(prod_low, k - 1)
                    if static is None or static >= 4:
                        pe.wait_ge(outb_ready, k - 3)
                    w = w2_hl[:].rearrange("i c h d -> i (c h d)")
                    for i in range(IC):
                        at_i = e2 * (2 * INNER) + 2 * i * P
                        for a, width in ((0, 2 * P), (1, P)) if i == 0 else ((1, P), (0, 2 * P)):
                            mm = pe.matmul(bank[6 + u][:, 0:width], (prod_hi, prod_lo)[a][:, u, i * P:(i + 1) * P],
                                           w[:, bass.ds(at_i, width)],
                                           start=(i == 0 and a == 0), stop=(i == IC - 1 and a == 0))
                    mm.then_inc(y_done, 1)
                if live(1):
                    pe.wait_ge(prod_ready, k)
                    for i in range(IC):
                        mm = pe.transpose(bank[4][:, i * P:(i + 1) * P], prod[:, 1 - u, i * P:(i + 1) * P], ident)
                    mm.then_inc(prod_turned, 1)

            load_expert(0, 0)
            turn_block(0, 0, 0)
            pipelined(pe, step, 2)

        @block.scalar
        def _(act):
            for i in range(STEPS):
                act.wait_ge(pre_ready, i + 1)
                act.activation(states[:, (i + 1) * COLS:(i + 2) * COLS], bank[i % 2][:, 0:COLS], ACT.Tanh
                               ).then_inc(state_ready, 1)
                j = i - HIGH_STEP
                if 0 <= j < 2 * EXPERTS:
                    if j == 0:
                        act.wait_ge(scales_ready, 1)
                    e = j % EXPERTS
                    cols = slice(e * INNER, (e + 1) * INNER)
                    if j < EXPERTS:
                        act.activation(w3_hl[:, 0, cols], w3_sb[:, cols], ACT.Copy, scale=scale[:, 1:2]).then_inc(w_high, 1)
                    else:
                        act.activation(w2_hl[:, e * IC:(e + 1) * IC, 0, :], w2_sb[:, cols].rearrange("i (c d) -> i c d", d=P),
                                       ACT.Copy, scale=scale[:, 2:3]).then_inc(w_high, 1)
                if i == STEPS - 2:
                    act.wait_ge(agree_ready, 1)
                    ok = act.value_load(agree_i[0:1, 0:1], min_val=0, max_val=1)
            with act.If(ok == 0):
                with act.Fori(0, CHUNKS) as c:
                    for p in range(CHUNK):
                        act.wait_ge(seq_pre, c * CHUNK + (p + 1))
                        act.activation(piece[:, p, :], bank[p % 2][:, 0:BATCH], ACT.Tanh).then_inc(seq_state, 1)
                    act.wait_ge(seq_state, c * CHUNK + (CHUNK + 1))
                    act.activation(states[:, MAIN:].rearrange("h (p k) -> h p k", k=COLS)[:, :, bass.ds(c * BATCH, BATCH)],
                                   piece[:], ACT.Copy).then_inc(seq_kept, 1)
                    act.wait_ge(seq_kept, c + 1)
            act.wait_ge(bg_ready, 1)
            for s in range(PAIRS + 3):
                if s < PAIRS:
                    n = s
                    act.wait_ge(wg_done, n + 1)
                    if n >= 2:
                        act.wait_ge(gated_ready, n - 1)
                    act.activation(gate_t[:, n % 2, :], bank[2 + n % 2][:, 0:PC], ACT.Tanh, bias=half_bg[:, 0:1], scale=0.5
                                   ).then_inc(tanh_ready, 1)
                if 0 <= s - 2 < PAIRS:
                    n = s - 2
                    act.wait_ge(norm2_ready, 2 * n + 2)
                    act.activation(rows[:, 2 * n:2 * n + 2, 0:P], norm2[:, ts4(n), :], ACT.Copy).then_inc(rows_high, 1)
                if s >= 3:
                    n = s - 3
                    act.wait_ge(rows_turned, n + 1)
                    act.activation(x_ffn[:, :, n * PC:(n + 1) * PC],
                                   bank[6][:].bitcast(F16)[:, 0:2 * PC].rearrange("d (h c) -> d h c", h=2), ACT.Copy
                                   ).then_inc(xffn_ready, 1)
            act.wait_ge(w_split, 3)
            for s in range(GROUPS * IC + 1):
                if s < GROUPS * IC:
                    n = s
                    act.wait_ge(up_done, n + 1)
                    if n >= GELUS:
                        act.wait_ge(act_low, n - GELUS + 1)
                    act.activation(gelu[:, n % GELUS, :], bank[n % 2][:], ACT.Gelu, scale=gelu_in).then_inc(gelu_done, 1)
                if s >= 1:
                    n = s - 1
                    g, i = divmod(n, IC)
                    act.wait_ge(gelu_done, n + 1)
                    if g >= 2:
                        act.wait_ge(down_done, g - 1)
                    act.activation(act_hi[:, g % 2, i, :], gelu[:, n % GELUS, :], ACT.Copy, scale=act_scale
                                   ).then_inc(act_high, 1)

            def take_turned(k, u):
                act.wait_ge(blk_turned, k + 1)
                act.activation(xblk_t[:, u, :], bank[5][:].bitcast(F16)[:, 0:2 * P], ACT.Copy).then_inc(xt_ready, 1)

            def step(k, v, static):
                live = lambda d: static is None or 0 <= static - d < BLOCKS
                u = v % 2
                if live(0):
                    act.wait_ge(h_done, k * 2 + 1)
                    if static is None or static >= 2:
                        act.wait_ge(prod_ready, k - 1)
                    act.activation(silu[:, u, :], bank[u][:], ACT.Silu, scale=silu_in).then_inc(silu_ready, 1)
                if live(-1):
                    take_turned(k + 1, 1 - u)
                if live(1):
                    act.wait_ge(prod_turned, k)
                    if static is None or static >= 3:
                        act.wait_ge(y_done, k - 2)
                    act.activation(prod_hi[:, 1 - u, :], bank[4][:], ACT.Copy).then_inc(prod_high, 1)

            take_turned(0, 0)
            pipelined(act, step, 1)

        @block.vector
        def _(dve):
            n_step = [0]

            def then_wait(ins):
                n_step[0] += 1
                ins.then_inc(dve_step, 1)
                dve.wait_ge(dve_step, n_step[0])

            dve.memset(states[:, 0:COLS], 0.0).then_inc(state_ready, 1)
            dve.memset(piece[:, CHUNK - 1, :], 0.0).then_inc(seq_state, 1)
            dve.memset(x_in[:].rearrange("h (p k) -> h p k", k=XW)[:, :, 0:PADC], 0.0).then_inc(pads_zero, 1)
            dve.wait_ge(small_in, 80)
            dve.tensor_scalar(half_bg[:], bg_sb[:], 0.5, None, ALU.mult).then_inc(bg_ready, 1)

            dve.tensor_copy(ident16[:], ident).then_inc(ident16_ready, 1)

            def statistics(src, st, mv, ve, tiles, ready, unit=1.0):
                for t in tiles:
                    ins = dve.bn_stats(st[:, t, :], src[:, t, :])
                then_wait(ins)
                for t in tiles:
                    ins = dve.bn_aggr(mv[:, t, :], st[:, t, :])
                then_wait(ins)
                ts = slice(tiles[0], tiles[-1] + 1)
                dve.tensor_scalar(ve[:, ts], mv[:, ts, 1], EPS, unit, ALU.add, ALU.mult).then_inc(ready, 1)

            def normalise(dst, src, mv, rs, tiles, n, ready):
                for i, t in enumerate(tiles):
                    dve.tensor_scalar(dst[:, n % 2 * 2 + i, :], src[:, t, :], mv[:, t, 0:1], rs[:, t:t + 1],
                                      ALU.subtract, ALU.mult).then_inc(ready, 1)

            def greatest(out_col, src):
                return dve.tensor_reduce(out_col, src, AX.X, ALU.max, apply_absolute_value=True)

            def greatest_part(j):
                dve.wait_ge(w_in[j], 16)
                return greatest(part_max[:, j // QUARTERS, j % QUARTERS:j % QUARTERS + 1],
                                (w1_sb, w3_sb, w2_sb)[j // QUARTERS][:, quarter(j)])

            for s in range(PAIRS + 2):
                if s < PAIRS:
                    dve.wait_ge(gathered[s], 32)
                    statistics(emb_rows, stats, meanvar, vareps, pair_tiles(s), var_ready)
                if s == 1:
                    dve.wait_ge(wgc_done, 1)
                    dve.tensor_copy(wgc[:], bank[4][:, 0:P]).then_inc(wgc_ready, 1)
                if 0 <= s - 1 < PAIRS:
                    dve.wait_ge(rstd_ready, s)
                    n = s - 1
                    normalise(norm_rows, emb_rows, meanvar, rstd, pair_tiles(n), n, norm_ready)
                    p0 = 2 * pair_tiles(n)[0]
                    dve.wait_ge(norm_turned, n + 1)
                    dve.tensor_copy(x_in[:, p0 * XW:(p0 + 4) * XW].rearrange("h (p k) -> h p k", k=XW)[:, :, PADC:XW],
                                    bank[2 + n % 2][:, 0:PC].rearrange("h (p k) -> h p k", k=COLS)).then_inc(x_ready, 1)
                if s >= 3:
                    greatest_part(s - 3)
            dve.wait_ge(sh_weights_in, 32)
            greatest(max_rows[:, 3:4], sw1_sb[:])
            greatest(max_rows[:, 4:5], sw2_sb[:])
            greatest(max_rows[:, 5:6], gate_sb[:])
            for j in range(PAIRS - 1, 3 * QUARTERS):
                ins = greatest_part(j)
            then_wait(ins)
            dve.tensor_reduce(max_rows[:, 0:3], part_max[:], AX.X, ALU.max).then_inc(max_ready, 1)
            dve.wait_ge(max_turned, 1)
            then_wait(dve.tensor_reduce(max_col[:], bank[5][0:WEIGHTS, 0:P], AX.X, ALU.max))
            dve.tensor_scalar(max_diag[:], ident[0:WEIGHTS, 0:WEIGHTS], max_col[:], None, ALU.mult).then_inc(diag_ready, 1)
            dve.wait_ge(max_spread, 1)
            then_wait(dve.tensor_copy(max_all[:], bank[6][:, 0:WEIGHTS]))
            then_wait(dve.tensor_scalar(max_exp[:], max_all[:].bitcast(I32), 0x7F800000, None, ALU.bitwise_and))
            then_wait(dve.tensor_scalar(max_exp_in[:], max_exp[:], float(97 << 23), float(167 << 23), ALU.max, ALU.min))
            then_wait(dve.tensor_scalar(scale_i[:], max_exp_in[:], -1.0, float(268 << 23), ALU.mult, ALU.add))
            then_wait(dve.tensor_scalar(unscale_i[:], scale_i[:], -1.0, float(254 << 23), ALU.mult, ALU.add))
            dve.tensor_scalar(silu_in, unscale[:, 0:1], 1 / X_SCALE, None, ALU.mult)
            dve.tensor_scalar(prod_scale, scale[:, 0:1], 2.0 ** -29 / X_SCALE, None, ALU.mult)
            dve.tensor_scalar(gelu_in, unscale[:, 3:4], 1 / X_SCALE, None, ALU.mult)
            dve.tensor_scalar(act_scale, scale[:, 3:4], 2.0 ** -7, None, ALU.mult)
            dve.tensor_tensor(inv_w1w3[:], unscale[:, 0:1], unscale[:, 1:2], ALU.mult)
            then_wait(dve.tensor_tensor(inv_sw[:], unscale[:, 3:4], unscale[:, 4:5], ALU.mult))
            then_wait(dve.tensor_tensor(inv_w1w3w2[:], inv_w1w3[:], unscale[:, 2:3], ALU.mult))
            dve.tensor_scalar(base_unscale, inv_sw[:], 2.0 ** 7, None, ALU.mult)
            then_wait(dve.tensor_scalar(y_unscale, inv_w1w3w2[:], 2.0 ** 29, None, ALU.mult))
            dve.tensor_copy(agree[:], ident[0:1, 0:1]).then_inc(scales_ready, 1)

            def low(lo, hi, w, c, ready):
                dve.scalar_tensor_tensor(out=lo, in0=w, scalar=scale[:, c:c + 1], in1=hi,
                                         op0=ALU.mult, op1=ALU.subtract).then_inc(ready, 1)

            for c, w, hl, ready in ((3, sw1_sb, sw1_hl, sh_split), (4, sw2_sb, sw2_hl, sh_split),
                                    (5, gate_sb, gate_hl, sh_split), (0, w1_sb, w1_hl, w_split)):
                then_wait(dve.tensor_scalar(hl[:, 0, :], w[:], scale[:, c:c + 1], None, ALU.mult))
                low(hl[:, 1, :], hl[:, 0, :], w[:], c, ready)
            dve.wait_ge(w_high, EXPERTS)
            low(w3_hl[:, 1, :], w3_hl[:, 0, :], w3_sb[:], 1, w_split)
            dve.wait_ge(w_high, 2 * EXPERTS)
            low(w2_hl[:, :, 1, :], w2_hl[:, :, 0, :], w2_sb[:].rearrange("i (c d) -> i c d", d=P), 2, w_split)

            met, last = (1 + WARM - MEET) * COLS, (1 + STEPS - MEET) * COLS
            dve.wait_ge(state_ready, 1 + STEPS - MEET)
            then_wait(dve.tensor_tensor(diff[:], states[:, met - COLS + BATCH:met],
                                        states[:, last - COLS:last - BATCH], ALU.subtract))
            then_wait(dve.tensor_tensor(diff2[:], diff[:], diff[:], ALU.mult))
            then_wait(dve.tensor_scalar(close[:], diff2[:], TOL * TOL, None, ALU.is_le))
            dve.tensor_reduce(close_row[:], close[:], AX.X, ALU.min).then_inc(close_ready, 1)
            dve.wait_ge(close_turned, 1)
            then_wait(dve.tensor_reduce(agree[:], bank[2][0:1, 0:P], AX.X, ALU.min))
            dve.tensor_copy(agree_i[:], agree[:]).then_inc(agree_ready, 1)

            for s in range(PAIRS + 2):
                if s < PAIRS:
                    n = s
                    dve.wait_ge(tanh_ready, n + 1)
                    dve.wait_ge(c_done, n + 1)
                    if n >= 2:
                        dve.wait_ge(wo_done, n - 1)
                    dve.scalar_tensor_tensor(out=gated[:, n % 2, :], in0=gate_t[:, n % 2, :], scalar=1.0,
                                             in1=bank[n % 2][:, 0:PC], op0=ALU.add, op1=ALU.mult).then_inc(gated_ready, 1)
                if 0 <= s - 1 < PAIRS:
                    n = s - 1
                    ts = slice(2 * n, 2 * n + 2)
                    dve.wait_ge(wo_done, n + 1)
                    dve.wait_ge(resid_ready, n // 2 + 1)
                    dve.scalar_tensor_tensor(out=attn_out[:, ts, :],
                                             in0=bank[4 + n % 2][:, 0:PC].rearrange("q (t d) -> q t d", t=2),
                                             scalar=0.5, in1=emb_rows[:, ts, :], op0=ALU.mult, op1=ALU.add
                                             ).then_inc(attn_ready, 1)
                    dve.wait_ge(attn_ready, n + 1)
                    statistics(attn_out, stats2, meanvar2, vareps2, (2 * n, 2 * n + 1), var2_ready, X_SCALE ** -2)
                if 0 <= s - 2 < PAIRS:
                    n = s - 2
                    dve.wait_ge(rstd2_ready, n + 1)
                    if n >= 2:
                        dve.wait_ge(rows_ready, n - 1)
                    normalise(norm2, attn_out, meanvar2, rstd2, (2 * n, 2 * n + 1), n, norm2_ready)

            te = lambda ap: ap.rearrange("q (t e) -> q t e", e=EXPERTS)
            et = lambda ap: ap.rearrange("q (e t) -> q t e", e=EXPERTS)
            over = lambda ap: ap.unsqueeze(2).to_broadcast([P, TILES, EXPERTS])
            rev = cst[:, C_REV:C_REV + ET]
            dve.wait_ge(logits_done, 1)
            then_wait(dve.tensor_reduce(te(logits[:]), bank[7][:, 0:2 * ET].rearrange("q (t h e) -> q t e h", h=2, e=EXPERTS),
                                        AX.X, ALU.add))
            then_wait(dve.tensor_reduce(top[:], te(logits[:]), AX.X, ALU.max))
            then_wait(dve.tensor_tensor(te(is_top[:]), te(logits[:]), over(top[:]), ALU.is_ge))
            then_wait(dve.tensor_tensor(rev_top[:], is_top[:], rev, ALU.mult))
            then_wait(dve.tensor_reduce(first_rev[:], te(rev_top[:]), AX.X, ALU.max))
            dve.tensor_tensor(et(onehot[:]), te(rev), over(first_rev[:]), ALU.is_equal).then_inc(onehot_ready, 1)
            dve.wait_ge(counts_done, 1)
            dve.wait_ge(onehot_ready, 1)
            then_wait(dve.tensor_tensor_scan(upto[:], cst[:, C_CARRY:C_CARRY + ET], bank[4][:, 0:ET], 0.0,
                                             ALU.mult, ALU.add))
            then_wait(dve.tensor_tensor(place[:], bank[5][:, 0:ET], upto[:], ALU.add))
            counts = upto[:].rearrange("q (e t) -> q e t", e=EXPERTS)[:, :, TILES - 1]
            then_wait(dve.tensor_scalar(blocks_i0[:], counts, float(P - 1), None, ALU.add))
            then_wait(dve.tensor_scalar(blocks_i[:], blocks_i0[:], 7, None, ALU.logical_shift_right))
            then_wait(dve.tensor_tensor_scan(blocks_end[:], cst[:, C_ONES:C_ONES + EXPERTS], blocks_i[:], 0.0,
                                             ALU.mult, ALU.add))
            then_wait(dve.tensor_tensor(blocks_start[:], blocks_end[:], blocks_i[:], ALU.subtract))
            e_t = lambda ap: ap.rearrange("q (e t) -> q e t", e=EXPERTS)
            then_wait(dve.scalar_tensor_tensor(out=e_t(place_all[:]),
                                               in0=blocks_start[:].unsqueeze(2).to_broadcast([P, EXPERTS, TILES]),
                                               scalar=float(P), in1=e_t(place[:]), op0=ALU.mult, op1=ALU.add))
            then_wait(dve.tensor_tensor(place_own[:], place_all[:], onehot[:], ALU.mult))
            then_wait(dve.tensor_reduce(slot_f[:], et(place_own[:]), AX.X, ALU.add))
            dve.tensor_copy(slot_i[:], slot_f[:]).then_inc(slots_ready, 1)
            k_e = lambda ap: ap.rearrange("q (k e) -> q k e", e=EXPERTS)
            then_wait(dve.tensor_tensor(k_e(past[:]), k_e(cst[0:1, C_BLOCK:C_BLOCK + BLOCKS * EXPERTS]),
                                        blocks_end[0:1, :].unsqueeze(1).to_broadcast([1, BLOCKS, EXPERTS]), ALU.is_ge))
            then_wait(dve.tensor_reduce(block_expert_f[:], k_e(past[:]), AX.X, ALU.add))
            dve.tensor_scalar(block_expert[:], block_expert_f[:], float(EXPERTS - 1), None, ALU.min
                              ).then_inc(experts_ready, 1)

            for g in range(GROUPS + 1):
                if g < GROUPS:
                    for i in range(IC):
                        n = g * IC + i
                        dve.wait_ge(act_high, n + 1)
                        if g >= 2:
                            dve.wait_ge(down_done, g - 1)
                        dve.scalar_tensor_tensor(out=act_lo[:, g % 2, i, :], in0=gelu[:, n % GELUS, :], scalar=act_scale,
                                                 in1=act_hi[:, g % 2, i, :], op0=ALU.mult, op1=ALU.subtract
                                                 ).then_inc(act_low, 1)
                if g == 0:
                    continue
                ts = slice(4 * g - 4, 4 * g)
                dve.wait_ge(down_done, g)
                dve.scalar_tensor_tensor(out=attn_out[:, ts, :],
                                         in0=bank[3 - g % 2][:].rearrange("q (t d) -> q t d", t=4),
                                         scalar=base_unscale, in1=attn_out[:, ts, :], op0=ALU.mult, op1=ALU.add
                                         ).then_inc(base_ready, 1)

            def step(k, v, static):
                live = lambda d: static is None or 0 <= static - d < BLOCKS
                u, w = v % 2, (v - 2) % RING
                if live(0):
                    dve.wait_ge(silu_ready, k + 1)
                    dve.wait_ge(h_done, k * 2 + 2)
                    if static is None or static >= 2:
                        dve.wait_ge(prod_turned, k - 1)
                    dve.scalar_tensor_tensor(out=prod[:, u, :], in0=bank[2 + u][:], scalar=prod_scale, in1=silu[:, u, :],
                                             op0=ALU.mult, op1=ALU.mult).then_inc(prod_ready, 1)
                if live(2):
                    dve.wait_ge(y_done, k - 1)
                    dve.wait_ge(res_in[w], ring_count(k - 2, w))
                    if static is None or static >= 2 + RING:
                        dve.wait_ge(out_stored[w], ring_count(k - 2 - RING, w))
                    dve.scalar_tensor_tensor(out=out_part[:, u, :], in0=bank[6 + u][:, P:2 * P], scalar=y_unscale,
                                             in1=res_blk[w][:], op0=ALU.mult, op1=ALU.add).then_inc(part_ready, 1)
                if live(1):
                    dve.wait_ge(prod_high, k)
                    dve.tensor_tensor(prod_lo[:, 1 - u, :], bank[4][:], prod_hi[:, 1 - u, :], ALU.subtract
                                      ).then_inc(prod_low, 1)
                if live(2):
                    dve.wait_ge(part_ready, k - 1)
                    dve.scalar_tensor_tensor(out=out_blk[w][:], in0=bank[6 + u][:, 0:P], scalar=y_unscale,
                                             in1=out_part[:, u, :], op0=ALU.mult, op1=ALU.add).then_inc(outb_ready, 1)

            pipelined(dve, step, 2)


_ARGS = ("tok", "ids", "consts", "emb", "sq", "bg", "bo", "gate", "w1", "w3", "w2", "sw1", "sw2")


def kernel(x, L0_tok_W, L0_attn_A, L0_attn_B, L0_attn_C, L0_attn_Wg, L0_attn_bg, L0_attn_Wo, L0_attn_bo,
           L0_ffn_gate_w, L0_ffn_w1, L0_ffn_w2, L0_ffn_w3, L0_ffn_sw1, L0_ffn_sw2):
    import concourse.bacc as bacc
    from concourse.bass_utils import run_bass_kernel_spmd

    row = np.ascontiguousarray
    tok = np.asarray(x).reshape(BATCH, CHUNKS, TILES, 2).transpose(3, 1, 0, 2).reshape(P, TILES)
    arrays = {
        "tok": row(tok),
        "ids": row_ids(),
        "consts": shape_constants(),
        "emb": row(np.asarray(L0_tok_W).T),
        "sq": row(np.stack([np.asarray(w).T for w in (L0_attn_A, L0_attn_B, L0_attn_C, L0_attn_Wg, L0_attn_Wo)]
                           + [np.asarray(L0_attn_C)], 1)),
        "bg": row(np.asarray(L0_attn_bg).reshape(P, 1)),
        "bo": row(np.asarray(L0_attn_bo).reshape(1, P)),
        "gate": row(np.asarray(L0_ffn_gate_w).T),
        "w1": row(np.asarray(L0_ffn_w1).transpose(2, 0, 1).reshape(P, EXPERTS * INNER)),
        "w3": row(np.asarray(L0_ffn_w3).transpose(2, 0, 1).reshape(P, EXPERTS * INNER)),
        "w2": row(np.asarray(L0_ffn_w2).reshape(EXPERTS, P, IC, P).transpose(3, 0, 2, 1).reshape(P, EXPERTS * INNER)),
        "sw1": row(np.asarray(L0_ffn_sw1).T),
        "sw2": row(np.asarray(L0_ffn_sw2).reshape(P, IC, P).transpose(2, 1, 0).reshape(P, INNER)),
    }
    nc = bacc.Bacc("TRN2", target_bir_lowering=False, num_devices=1)
    aps = [nc.dram_tensor(n, arrays[n].shape, mybir.dt.from_np(arrays[n].dtype), kind="ExternalInput").ap()
           for n in _ARGS]
    out = nc.dram_tensor("out", (BATCH * SEQ, P), F32, kind="ExternalOutput").ap()
    dispatch = nc.dram_tensor("dispatch", (BLOCKS * P, ROW), F16).ap()
    resid = nc.dram_tensor("resid", (TILES * P, P), F32).ap()
    build(nc, *aps, out, dispatch, resid)
    got = run_bass_kernel_spmd(nc, [arrays], core_ids=[0])
    return got.results[0]["out"].reshape(BATCH, SEQ, P)
```

```python
from contextlib import ExitStack

import numpy as np
import concourse.bass as bass
from concourse import mybir

P = 128
BATCH, SEQ = 4, 512
EXPERTS, INNER = 8, 512
CHUNK = 16
CHUNKS = SEQ // CHUNK
WARM = 40
MEET = 5
COLS = CHUNKS * BATCH
PADC = -(-WARM // CHUNK) * BATCH
XW = COLS + PADC
STEPS = WARM + CHUNK
MAIN = (1 + WARM) * COLS
TILES = BATCH * SEQ // P
GROUPS = TILES // 4
GC = 4 * P
PPT = P // COLS
PPP = 2 * PPT
PAIRS = TILES // 2
PC = 2 * P
MAX_STEP = 32
HIGH_STEP = MAX_STEP + 6
FIRST_TILE = -WARM % CHUNK // PPT
IC = INNER // P
PARTS = 8
GELUS = 8
WEIGHTS = 6
BLOCKS = TILES + EXPERTS - 1
ROW = 2 * P + 4
NO_ROW = 4096
RING = 4
FEW = BLOCKS // RING * RING
X_SCALE = 2.0 ** 8
EPS = 1e-5
TOL = 2.0 ** -18

F32 = mybir.dt.float32
I32 = mybir.dt.int32
F16 = mybir.dt.float16
ALU = mybir.AluOpType
ACT = mybir.ActivationFunctionType
AX = mybir.AxisListType

C_IDENT, C_RANK, C_ONES, C_REV, C_CARRY, C_BLOCK, C_POW = 0, 128, 256, 384, 512, 640, 824
C_END = 840


def shape_constants():
    c = np.zeros((P, C_END), np.float32)
    j = np.arange(P)
    c[:, C_IDENT:C_IDENT + P] = np.eye(P)
    c[:, C_RANK:C_RANK + P] = -(j[:, None] >= j[None, :]).astype(np.float32)
    c[:, C_ONES:C_ONES + P] = 1.0
    c[:, C_REV:C_REV + P] = np.tile(EXPERTS - np.arange(EXPERTS), TILES)
    c[:, C_CARRY:C_CARRY + P] = np.tile(np.arange(TILES) > 0, EXPERTS)
    c[:, C_BLOCK:C_BLOCK + BLOCKS * EXPERTS] = np.repeat(np.arange(BLOCKS), EXPERTS)
    c[:, C_POW:C_POW + TILES] = -0.5
    return c


def row_ids():
    q, t = np.arange(P)[:, None], np.arange(TILES)[None, :]
    pos = (q // BATCH % CHUNKS) * CHUNK + PPT * t + q // COLS
    return np.stack([(q % BATCH) * SEQ + pos, t * P + q], -1).astype(np.int32)


def build(nc, tok, ids, consts, emb, sq, bg, bo, gate, w1, w3, w2, sw1, sw2, out, dispatch, resid):
    with ExitStack() as ctx:
        def sb(name, shape, dt=F32):
            return ctx.enter_context(nc.sbuf_tensor(name, shape, dt))

        def sem(name):
            return ctx.enter_context(nc.semaphore(name))

        bank = [ctx.enter_context(nc.psum_tensor(f"bank{i}", [P, 512], F32)) for i in range(8)]

        turned = (bank[4], bank[7])

        tok_sb = sb("tok_sb", [P, TILES], I32)
        cst = sb("cst", [P, C_END])
        sq_sb = sb("sq_sb", [P, 6, P])
        bg_sb = sb("bg_sb", [P, 1])
        half_bg = sb("half_bg", [P, 1])
        bo_sb = sb("bo_sb", [P, P])
        gate_sb = sb("gate_sb", [P, EXPERTS])
        w1_hl, w3_hl = (sb(n, [P, 2, EXPERTS * INNER], F16) for n in ("w1_hl", "w3_hl"))
        w2_hl = sb("w2_hl", [P, EXPERTS * IC, 2, P], F16)
        sw1_hl, sw2_hl = (sb(n, [P, 2, INNER], F16) for n in ("sw1_hl", "sw2_hl"))
        gate_hl = sb("gate_hl", [P, 2, EXPERTS], F16)
        part_max = sb("part_max", [P, 3, PARTS])
        max_rows = sb("max_rows", [P, WEIGHTS])
        max_col = sb("max_col", [WEIGHTS, 1])
        max_diag = sb("max_diag", [WEIGHTS, WEIGHTS])
        max_all = sb("max_all", [P, WEIGHTS])
        max_exp, max_exp_in = (sb(n, [P, WEIGHTS], I32) for n in ("max_exp", "max_exp_in"))
        scale_i, unscale_i = (sb(n, [P, WEIGHTS], I32) for n in ("scale_i", "unscale_i"))
        factor = sb("factor", [P, 6])
        inv_w1w3, inv_w1w3w2, inv_sw = (sb(n, [P, 1]) for n in ("inv_w1w3", "inv_w1w3w2", "inv_sw"))
        ident16 = sb("ident16", [P, P], F16)
        w1_sb = sb("w1_sb", [P, EXPERTS * INNER])
        w3_sb = sb("w3_sb", [P, EXPERTS * INNER])
        w2_sb = sb("w2_sb", [P, EXPERTS * INNER])
        sw1_sb = sb("sw1_sb", [P, INNER])
        sw2_sb = sb("sw2_sb", [P, INNER])
        ident = cst[:, C_IDENT:C_IDENT + P]
        ones = cst[:, C_ONES:C_ONES + P]
        at, bt, ct, wgt, wot, c_nat = (sq_sb[:, i, :] for i in range(6))

        emb_rows = sb("emb_rows", [P, TILES, P])
        stats = sb("stats", [P, TILES, 6])
        meanvar = sb("meanvar", [P, TILES, 2])
        vareps = sb("vareps", [P, TILES])
        rstd = sb("rstd", [P, TILES])
        norm_rows = sb("norm_rows", [P, 4, P])
        x_in = sb("x_in", [P, CHUNK * XW])

        states = sb("states", [P, (1 + STEPS) * COLS])
        piece = sb("piece", [P, CHUNK, BATCH])
        diff = sb("diff", [P, COLS - BATCH])
        diff2 = sb("diff2", [P, COLS - BATCH])
        close = sb("close", [P, COLS - BATCH])
        close_row = sb("close_row", [P, 1])
        agree = sb("agree", [1, 1])
        agree_i = sb("agree_i", [1, 1], I32)

        wgc = sb("wgc", [P, P])
        gate_t = sb("gate_t", [P, 2, PC])
        gated = sb("gated", [P, 2, PC])
        attn_out = sb("attn_out", [P, TILES, P])
        stats2 = sb("stats2", [P, TILES, 6])
        meanvar2 = sb("meanvar2", [P, TILES, 2])
        vareps2 = sb("vareps2", [P, TILES])
        rstd2 = sb("rstd2", [P, TILES])
        norm2 = sb("norm2", [P, 4, P])
        rows = sb("rows", [P, TILES, ROW], F16)
        x_ffn = sb("x_ffn", [P, 2, TILES * P], F16)

        ET = EXPERTS * TILES
        logits = sb("logits", [P, ET])
        top = sb("top", [P, TILES])
        is_top = sb("is_top", [P, ET])
        rev_top = sb("rev_top", [P, ET])
        first_rev = sb("first_rev", [P, TILES])
        onehot = sb("onehot", [P, ET])
        upto = sb("upto", [P, ET])
        place = sb("place", [P, ET])
        place_all = sb("place_all", [P, ET])
        place_own = sb("place_own", [P, ET])
        blocks_i0 = sb("blocks_i0", [P, EXPERTS], I32)
        blocks_i = sb("blocks_i", [P, EXPERTS], I32)
        blocks_end = sb("blocks_end", [P, EXPERTS])
        blocks_start = sb("blocks_start", [P, EXPERTS])
        slot_f = sb("slot_f", [P, TILES])
        slot_i = sb("slot_i", [P, TILES], I32)
        past = sb("past", [1, BLOCKS * EXPERTS])
        block_expert_f = sb("block_expert_f", [1, BLOCKS])
        block_expert = sb("block_expert", [1, BLOCKS], I32)
        few_blocks = sb("few_blocks", [1, 1], I32)
        fill = sb("fill", [P, ROW], F16)
        ids_all = sb("ids_all", [P, BLOCKS, 4], F16)

        gelu = w1_sb[:].rearrange("i (n j) -> i n j", n=GELUS)
        act_hi, act_lo = (w[:, 0:TILES * P * IC // 2].bitcast(F16).rearrange("i (g n j) -> i g n j", g=GROUPS, n=IC)
                          for w in (states, w3_sb))

        xblk = sb("xblk", [P, RING, 2 * P], F16)
        xblk_t = sb("xblk_t", [P, 2, 2 * P], F16)
        silu, prod = (w3_sb[:, i * 2 * INNER:(i + 1) * 2 * INNER].rearrange("i (u j) -> i u j", u=2) for i in range(2))
        out_part = sb("out_part", [P, 2, P])
        prod_hi, prod_lo = (w1_sb[:, i * INNER:(i + 1) * INNER].bitcast(F16).rearrange("i (u j) -> i u j", u=2)
                            for i in range(2))
        idb = [sb(f"idb{i}", [P, 2], I32) for i in range(RING)]
        res_blk = [sb(f"res_blk{i}", [P, P]) for i in range(RING)]
        out_blk = [sb(f"out_blk{i}", [P, P]) for i in range(RING)]

        tok_in, small_in = sem("tok_in"), sem("small_in")
        w_in = [sem(f"w_in{j}") for j in range(3 * PARTS)]
        max_ready, max_turned, diag_ready, max_spread, scales_ready, ident16_ready = (
            sem(n) for n in ("max_ready", "max_turned", "diag_ready", "max_spread", "scales_ready", "ident16_ready"))
        w_high, sh_split, w_split = sem("w_high"), sem("sh_split"), sem("w_split")
        sh_weights_in = sem("sh_weights_in")
        ids_in, filled, fill_stored = sem("ids_in"), sem("filled"), sem("fill_stored")
        gathered = [sem(f"gathered{n}") for n in range(PAIRS)]
        dve_step = sem("dve_step")
        var_ready, rstd_ready, norm_ready = sem("var_ready"), sem("rstd_ready"), sem("norm_ready")
        norm_turned, x_ready, pads_zero = sem("norm_turned"), sem("x_ready"), sem("pads_zero")
        pre_ready, state_ready = sem("pre_ready"), sem("state_ready")
        close_ready, close_turned, agree_ready = sem("close_ready"), sem("close_turned"), sem("agree_ready")
        seq_pre, seq_state, seq_kept = sem("seq_pre"), sem("seq_state"), sem("seq_kept")
        bg_ready, resid_ready = sem("bg_ready"), sem("resid_ready")
        wgc_done, wgc_ready, c_done, wg_done, tanh_ready, gated_ready, wo_done, attn_ready = (
            sem(n) for n in ("wgc_done", "wgc_ready", "c_done", "wg_done", "tanh_ready", "gated_ready", "wo_done",
                             "attn_ready"))
        var2_ready, rstd2_ready, rows_ready, rows_turned, xffn_ready, logits_done = (
            sem(n) for n in ("var2_ready", "rstd2_ready", "rows_ready", "rows_turned", "xffn_ready", "logits_done"))
        norm2_ready, rows_high = sem("norm2_ready"), sem("rows_high")
        onehot_ready, counts_done, slots_ready, experts_ready = (
            sem(n) for n in ("onehot_ready", "counts_done", "slots_ready", "experts_ready"))
        dispatched = sem("dispatched")
        up_done, gelu_done, act_high, down_done, base_ready, base_stored = (
            sem(n) for n in ("up_done", "gelu_done", "act_high", "down_done", "base_ready", "base_stored"))
        act_low = sem("act_low")
        all_ids_in = sem("all_ids_in")
        xblk_in = [sem(f"xblk_in{i}") for i in range(RING)]
        res_in = [sem(f"res_in{i}") for i in range(RING)]
        out_stored = [sem(f"out_stored{i}") for i in range(RING)]
        id_copied, blk_turned, xt_ready, h_done, silu_ready, prod_ready = (
            sem(n) for n in ("id_copied", "blk_turned", "xt_ready", "h_done", "silu_ready", "prod_ready"))
        prod_turned, prod_high, prod_low, y_done, part_ready, outb_ready = (
            sem(n) for n in ("prod_turned", "prod_high", "prod_low", "y_done", "part_ready", "outb_ready"))
        res_zero, first_id_copied = sem("res_zero"), sem("first_id_copied")

        block = ctx.enter_context(nc.Block())

        def pipelined(eng, body, lag, at_end=None):
            eng.wait_ge(experts_ready, 1)
            few = eng.value_load(few_blocks[0:1, 0:1], min_val=0, max_val=1)
            lo = RING
            hi = lo + (BLOCKS - lo) // RING * RING
            assert hi == FEW
            for k in range(lo):
                body(k, k % RING, k, BLOCKS)
            with eng.Fori(0, (hi - lo) // RING) as m:
                for v in range(RING):
                    body(m * RING + (lo + v), v, None, BLOCKS)
            for is_few, end in ((0, BLOCKS), (1, FEW)):
                with eng.If(few == is_few):
                    for k in range(hi, end + lag):
                        body(k, k % RING, k, end)
                    if at_end:
                        at_end(end)

        def pair_tiles(n):
            t = (FIRST_TILE + 2 * n) % TILES
            return (t, t + 1)

        def part(j):
            width = EXPERTS * INNER // PARTS
            return slice(j % PARTS * width, (j % PARTS + 1) * width)

        def ts4(n):
            return slice(n % 2 * 2, n % 2 * 2 + 2)

        def ring_count(k, v):
            return (k - v) * (16 // RING) + 16

        scale, unscale = scale_i[:].bitcast(F32), unscale_i[:].bitcast(F32)
        silu_in, prod_scale, y_unscale, gelu_in, act_scale, base_unscale = (factor[:, i:i + 1] for i in range(6))

        @block.sync
        def _(sp):
            def store_base(g):
                sp.wait_ge(base_ready, g + 1)
                sp.dma_start(resid.rearrange("(t p) d -> p t d", p=P)[:, 4 * g:4 * g + 4, :],
                             attn_out[:, 4 * g:4 * g + 4, :]).then_inc(base_stored, 16)

            def load_block(k, v, static):
                if static is None or static >= RING:
                    sp.wait_ge(blk_turned, k - (RING - 1))
                sp.dma_start(xblk[:, v, :], dispatch[bass.ds(k * P, P), 0:2 * P]).then_inc(xblk_in[v], 16)

            sp.dma_start(tok_sb[:], tok).then_inc(tok_in, 16)
            sp.dma_start(cst[:], consts).then_inc(small_in, 16)
            sp.dma_start(sq_sb[:], sq).then_inc(small_in, 16)
            sp.dma_start(bg_sb[:], bg).then_inc(small_in, 16)
            sp.dma_start(bo_sb[:], bo.to_broadcast([P, P])).then_inc(small_in, 16)
            sp.dma_start(gate_sb[:], gate).then_inc(small_in, 16)
            sp.dma_start(rows[:].bitcast(I32)[:, :, P:P + 2], ids).then_inc(ids_in, 16)
            sp.wait_ge(gathered[0], 32)
            sp.dma_start(sw1_sb[:], sw1).then_inc(sh_weights_in, 16)
            sp.dma_start(sw2_sb[:], sw2).then_inc(sh_weights_in, 16)
            for j in range(3 * PARTS):
                if 1 + j < PAIRS:
                    sp.wait_ge(gathered[1 + j], 32)
                w_sb, w = ((w1_sb, w1), (w3_sb, w3), (w2_sb, w2))[j // PARTS]
                sp.dma_start(w_sb[:, part(j)], w[:, part(j)]).then_inc(w_in[j], 16)
            sp.wait_ge(filled, 2)
            sp.dma_start(dispatch.rearrange("(k p) c -> p k c", p=P),
                         fill[:].unsqueeze(1).to_broadcast([P, BLOCKS, ROW])).then_inc(fill_stored, 16)
            for g in range(GROUPS - 1):
                store_base(g)
            sp.wait_ge(dispatched, 16 * TILES)
            load_block(0, 0, 0)
            sp.dma_start(ids_all[:], dispatch.rearrange("(k p) c -> p k c", p=P)[:, :, 2 * P:ROW]).then_inc(all_ids_in, 16)
            load_block(1, 1, 1)
            store_base(GROUPS - 1)
            for k in range(2, RING):
                load_block(k, k, k)
            with sp.Fori(0, BLOCKS // RING - 1) as m:
                for v in range(RING):
                    load_block(m * RING + (RING + v), v, None)
            for k in range(BLOCKS // RING * RING, BLOCKS):
                load_block(k, k % RING, k)
            for v in range(RING):
                sp.wait_ge(xblk_in[v], 16 * len(range(v, BLOCKS, RING)))

        @block.gpsimd
        def _(pool):
            pool.memset(fill[:, 0:2 * P], 0.0).then_inc(filled, 1)
            pool.memset(fill[:].bitcast(I32)[:, P:P + 2], NO_ROW).then_inc(filled, 1)
            pool.wait_ge(tok_in, 16)
            for n in range(PAIRS + 2):
                if n < PAIRS:
                    for t in pair_tiles(n):
                        pool.indirect_dma_start(out=emb_rows[:, t, :], out_offset=None, in_=emb,
                                                in_offset=bass.IndirectOffsetOnAxis(ap=tok_sb[:, t:t + 1], axis=0),
                                                ).then_inc(gathered[n], 16)
                if n >= 2:
                    t0 = pair_tiles(n - 2)[0]
                    if n == 2:
                        pool.wait_ge(small_in, 80)
                    pool.wait_ge(var_ready, n - 1)
                    pool.tensor_tensor(rstd[:, t0:t0 + 2], vareps[:, t0:t0 + 2], cst[:, C_POW:C_POW + 2], ALU.pow
                                       ).then_inc(rstd_ready, 1)
            pool.wait_ge(norm_ready, TILES)
            for g in range(GROUPS):
                ts = slice(4 * g, 4 * g + 4)
                pool.tensor_tensor(emb_rows[:, ts, :], emb_rows[:, ts, :],
                                   bo_sb[:].unsqueeze(1).to_broadcast([P, 4, P]), ALU.add).then_inc(resid_ready, 1)
            for i in range(RING):
                pool.memset(res_blk[i][:], 0.0).then_inc(res_zero, 1)
            for s in range(PAIRS + 1):
                if s < PAIRS:
                    ts = slice(2 * s, 2 * s + 2)
                    pool.wait_ge(var2_ready, s + 1)
                    pool.tensor_tensor(rstd2[:, ts], vareps2[:, ts], cst[:, C_POW:C_POW + 2], ALU.pow
                                       ).then_inc(rstd2_ready, 1)
                if s >= 1:
                    n = s - 1
                    ts = slice(2 * n, 2 * n + 2)
                    pool.wait_ge(rows_high, n + 1)
                    pool.tensor_tensor(rows[:, ts, P:2 * P], norm2[:, ts4(n), :], rows[:, ts, 0:P], ALU.subtract
                                       ).then_inc(rows_ready, 1)
            pool.wait_ge(fill_stored, 16)
            pool.wait_ge(ids_in, 16)
            pool.wait_ge(rows_ready, PAIRS)
            pool.wait_ge(slots_ready, 1)
            for t in range(TILES):
                pool.indirect_dma_start(out=dispatch, out_offset=bass.IndirectOffsetOnAxis(ap=slot_i[:, t:t + 1], axis=0),
                                        in_=rows[:, t, :], in_offset=None).then_inc(dispatched, 16)
            pool.wait_ge(all_ids_in, 16)
            pool.wait_ge(res_zero, RING)
            last_row = pool.to_reg(TILES * P - 1)

            def step(k, v, static, end):
                if static is None:
                    pool.wait_ge(id_copied, k - 1)
                if static is None or static < end:
                    if static is None or static >= RING:
                        pool.wait_ge(out_stored[v], ring_count(k - RING, v))
                    pool.tensor_copy(idb[v][:], ids_all[:].bitcast(I32).rearrange("p k c -> p (k c)")[:, bass.ds(k * 2, 2)]
                                     ).then_inc(first_id_copied if static == 0 else id_copied, 1)
                    pool.wait_ge(base_stored, 16 * GROUPS)
                    if static == 0:
                        pool.wait_ge(first_id_copied, 1)
                    else:
                        pool.wait_ge(id_copied, k)
                    pool.indirect_dma_start(out=res_blk[v][:], out_offset=None, in_=resid,
                                            in_offset=bass.IndirectOffsetOnAxis(ap=idb[v][:, 1:2], axis=0),
                                            bounds_check=last_row, oob_is_err=False).then_inc(res_in[v], 16)
                if static is None or 2 <= static:
                    w = (v - 2) % RING
                    pool.wait_ge(all_ids_in, 16)
                    pool.wait_ge(outb_ready, k - 1)
                    pool.indirect_dma_start(out=out, out_offset=bass.IndirectOffsetOnAxis(ap=idb[w][:, 0:1], axis=0),
                                            in_=out_blk[w][:], in_offset=None,
                                            bounds_check=last_row, oob_is_err=False).then_inc(out_stored[w], 16)

            def all_stored(end):
                for v in range(RING):
                    pool.wait_ge(out_stored[v], 16 * len(range(v, end, RING)))

            pipelined(pool, step, 2, all_stored)

        @block.tensor
        def _(pe):
            pe.wait_ge(small_in, 80)
            pe.matmul(bank[4][:, 0:P], c_nat, wgt, start=True, stop=True).then_inc(wgc_done, 1)

            def turn_pair(n):
                if n >= 2:
                    pe.wait_ge(x_ready, n - 1)
                for i in range(2):
                    pe.wait_ge(norm_ready, 2 * n + i + 1)
                    mm = pe.transpose(bank[2 + n % 2][:, i * P:(i + 1) * P], norm_rows[:, n % 2 * 2 + i, :], ident)
                mm.then_inc(norm_turned, 1)

            turn_pair(0)
            pe.wait_ge(pads_zero, 1)
            for i in range(STEPS):
                if i < CHUNK and i % PPP == 0:
                    pe.wait_ge(x_ready, i // PPP + 1)
                shift = -((i - WARM) // CHUNK)
                p = (i - WARM) % CHUNK
                x_at = p * XW + PADC - shift * BATCH
                pre = bank[i % 2][:, 0:COLS]
                pe.matmul(pre, bt, x_in[:, x_at:x_at + COLS], start=True, stop=False)
                pe.wait_ge(state_ready, i + 1)
                pe.matmul(pre, at, states[:, i * COLS:(i + 1) * COLS], start=False, stop=True).then_inc(pre_ready, 1)
                if i % PPP == 0 and i // PPP + 1 < PAIRS:
                    turn_pair(i // PPP + 1)
                if i == MAX_STEP:
                    pe.wait_ge(max_ready, 1)
                    pe.transpose(bank[5][0:WEIGHTS, 0:P], max_rows[:], ident).then_inc(max_turned, 1)
                if i == MAX_STEP + 2:
                    pe.wait_ge(diag_ready, 1)
                    pe.matmul(bank[6][:, 0:WEIGHTS], ones[0:WEIGHTS, :], max_diag[:], start=True, stop=True
                              ).then_inc(max_spread, 1)
                if i == STEPS - 3:
                    pe.wait_ge(close_ready, 1)
                    pe.transpose(bank[2][0:1, 0:P], close_row[:, 0:1], ident).then_inc(close_turned, 1)
                if i == STEPS - 2:
                    pe.wait_ge(agree_ready, 1)
                    ok = pe.value_load(agree_i[0:1, 0:1], min_val=0, max_val=1)

            with pe.If(ok == 0):
                pe.wait_ge(state_ready, 1 + STEPS)
                with pe.Fori(0, CHUNKS) as c:
                    for p in range(CHUNK):
                        pre = bank[p % 2][:, 0:BATCH]
                        pe.matmul(pre, bt, x_in[:, bass.ds(c * BATCH + (p * XW + PADC), BATCH)], start=True, stop=False)
                        pe.wait_ge(seq_state, c * CHUNK + (p + 1))
                        pe.matmul(pre, at, piece[:, (p - 1) % CHUNK, :], start=False, stop=True).then_inc(seq_pre, 1)
                pe.wait_ge(seq_kept, CHUNKS)

            pe.wait_ge(wgc_ready, 1)
            pe.wait_ge(ident16_ready, 1)
            pe.wait_ge(sh_split, 3)
            pe.wait_ge(state_ready, 1 + STEPS)

            def kept(n):
                return states[:, MAIN + n * PC:MAIN + (n + 1) * PC]

            def gate(n):
                if n >= 2:
                    pe.wait_ge(tanh_ready, n - 1)
                pe.matmul(bank[2 + n % 2][:, 0:PC], wgc[:], kept(n), start=True, stop=True).then_inc(wg_done, 1)

            halves = ((0, 0), (0, 1), (1, 0))

            def up(n):
                g, i = divmod(n, IC)
                if n >= 2:
                    pe.wait_ge(gelu_done, n - 1)
                for j, (a, b) in enumerate(halves):
                    mm = pe.matmul(bank[n % 2][:], sw1_hl[:, a, i * P:(i + 1) * P], x_ffn[:, b, g * GC:(g + 1) * GC],
                                   start=(j == 0), stop=(j == 2))
                mm.then_inc(up_done, 1)

            gate(0)
            for s in range(PAIRS + 5):
                if s < PAIRS:
                    n = s
                    if n >= 2:
                        pe.wait_ge(gated_ready, n - 1)
                    pe.matmul(bank[n % 2][:, 0:PC], ct, kept(n), start=True, stop=True).then_inc(c_done, 1)
                if s + 1 < PAIRS:
                    gate(s + 1)
                if 0 <= s - 1 < PAIRS:
                    n = s - 1
                    pe.wait_ge(gated_ready, n + 1)
                    if n >= 2:
                        pe.wait_ge(attn_ready, n - 1)
                    for i in range(2):
                        mm = pe.matmul(bank[4 + n % 2][:, i * P:(i + 1) * P], gated[:, n % 2, i * P:(i + 1) * P], wot,
                                       start=True, stop=True)
                    mm.then_inc(wo_done, 1)
                if 0 <= s - 4 < PAIRS:
                    n = s - 4
                    if n >= 1:
                        pe.wait_ge(xffn_ready, n)
                    pe.wait_ge(rows_ready, n + 1)
                    for h in range(2):
                        for i in range(2):
                            mm = pe.transpose(bank[6][:].bitcast(F16)[:, (2 * h + i) * P:(2 * h + i + 1) * P],
                                              rows[:, 2 * n + i, h * P:(h + 1) * P], ident16[:])
                    mm.then_inc(rows_turned, 1)
                if 0 <= s - 5 < PAIRS:
                    n = s - 5
                    pe.wait_ge(xffn_ready, n + 1)
                    for t in range(2 * n, 2 * n + 2):
                        for h in range(2):
                            mm = pe.matmul(bank[7][:, t * 2 * EXPERTS:(t + 1) * 2 * EXPERTS],
                                           x_ffn[:, h, t * P:(t + 1) * P], gate_hl[:].rearrange("d h e -> d (h e)"),
                                           start=(h == 0), stop=(h == 1))
                    if n == PAIRS - 1:
                        mm.then_inc(logits_done, 1)
                if PAIRS <= s < PAIRS + 2:
                    if s == PAIRS:
                        pe.wait_ge(gated_ready, PAIRS)
                    up(s - PAIRS)

            def down(m):
                g, t = divmod(m, 4)
                if t == 0:
                    pe.wait_ge(act_low, (g + 1) * IC)
                    if g >= 2:
                        pe.wait_ge(base_ready, g - 1)
                for i in range(IC):
                    for j, (a, b) in enumerate(halves):
                        mm = pe.matmul(bank[2 + g % 2][:, t * P:(t + 1) * P],
                                       (act_hi, act_lo)[a][:, g, i, t * P:(t + 1) * P],
                                       sw2_hl[:, b, i * P:(i + 1) * P],
                                       start=(i == 0 and j == 0), stop=(i == IC - 1 and j == 2))
                if t == 3:
                    mm.then_inc(down_done, 1)

            up(2)
            up(3)
            pe.wait_ge(onehot_ready, 1)
            pe.matmul(bank[4][:, 0:P], ones, onehot[:], start=True, stop=True)
            pe.matmul(bank[5][:, 0:P], cst[:, C_RANK:C_RANK + P], onehot[:], start=True, stop=True).then_inc(counts_done, 1)
            for n in range(4, 2 * IC):
                up(n)
            for m in range(TILES):
                if m + 2 * IC < GROUPS * IC:
                    up(m + 2 * IC)
                down(m)

            pe.wait_ge(w_split, 3)
            pe.wait_ge(experts_ready, 1)
            pe.wait_ge(base_ready, GROUPS - 1)

            def turn_block(k, v, static):
                pe.wait_ge(xblk_in[v], ring_count(k, v))
                if static is None or static >= 1:
                    pe.wait_ge(xt_ready, k)
                for h in range(2):
                    mm = pe.transpose(bank[5][:].bitcast(F16)[:, h * P:(h + 1) * P], xblk[:, v, h * P:(h + 1) * P],
                                      ident16[:])
                mm.then_inc(blk_turned, 1)

            expert_of = [pe.alloc_register(f"expert_of{v}") for v in range(RING)]

            def load_expert(k, v):
                pe.reg_load(expert_of[v], block_expert[0:1, bass.ds(k, 1)])

            def step(k, v, static, end):
                live = lambda d: static is None or 0 <= static - d < end
                u = v % 2
                if live(0):
                    e = pe.snap(expert_of[v], min_val=0, max_val=EXPERTS - 1)
                    pe.wait_ge(xt_ready, k + 1)
                    if static == 1:
                        pe.wait_ge(base_ready, GROUPS)
                    if static is None or static >= 2:
                        pe.wait_ge(prod_ready, k - 1)
                    for w_hl, hb in ((w1_hl, bank[u]), (w3_hl, bank[2 + u])):
                        w = w_hl[:].rearrange("d h c -> d (h c)")
                        for j, (a, b) in enumerate(halves):
                            mm = pe.matmul(hb[:], xblk_t[:, u, b * P:(b + 1) * P],
                                           w[:, bass.ds(e * INNER + a * EXPERTS * INNER, INNER)],
                                           start=(j == 0), stop=(j == 2))
                        mm.then_inc(h_done, 1)
                if live(-1):
                    load_expert(k + 1, (v + 1) % RING)
                    turn_block(k + 1, (v + 1) % RING, None if static is None else static + 1)
                if live(1):
                    pe.wait_ge(prod_ready, k)
                    if static is None or static >= 3:
                        pe.wait_ge(prod_low, k - 2)
                    for i in range(IC):
                        mm = pe.transpose(turned[1 - u][:, i * P:(i + 1) * P], prod[:, 1 - u, i * P:(i + 1) * P], ident)
                    mm.then_inc(prod_turned, 1)
                if live(2):
                    e2 = pe.snap(expert_of[(v - 2) % RING], min_val=0, max_val=EXPERTS - 1)
                    pe.wait_ge(prod_low, k - 1)
                    if static is None or static >= 3:
                        pe.wait_ge(outb_ready, k - 2)
                    w = w2_hl[:].rearrange("i c h d -> i (c h d)")
                    for i in range(IC):
                        at_i = e2 * (2 * INNER) + 2 * i * P
                        for a, width in ((0, 2 * P), (1, P)) if i == 0 else ((1, P), (0, 2 * P)):
                            mm = pe.matmul(bank[6][:, 0:width], (prod_hi, prod_lo)[a][:, u, i * P:(i + 1) * P],
                                           w[:, bass.ds(at_i, width)],
                                           start=(i == 0 and a == 0), stop=(i == IC - 1 and a == 0))
                    mm.then_inc(y_done, 1)

            load_expert(0, 0)
            turn_block(0, 0, 0)
            pipelined(pe, step, 2)

        @block.scalar
        def _(act):
            for i in range(STEPS):
                act.wait_ge(pre_ready, i + 1)
                act.activation(states[:, (i + 1) * COLS:(i + 2) * COLS], bank[i % 2][:, 0:COLS], ACT.Tanh
                               ).then_inc(state_ready, 1)
                j = i - HIGH_STEP
                if 0 <= j < 2 * EXPERTS:
                    if j == 0:
                        act.wait_ge(scales_ready, 1)
                    e = j % EXPERTS
                    cols = slice(e * INNER, (e + 1) * INNER)
                    if j < EXPERTS:
                        act.activation(w3_hl[:, 0, cols], w3_sb[:, cols], ACT.Copy, scale=scale[:, 1:2]).then_inc(w_high, 1)
                    else:
                        act.activation(w2_hl[:, e * IC:(e + 1) * IC, 0, :],
                                       w2_sb[:, cols].rearrange("i (c d) -> i c d", d=P), ACT.Copy, scale=scale[:, 2:3]).then_inc(w_high, 1)
                if i == STEPS - 2:
                    act.wait_ge(agree_ready, 1)
                    ok = act.value_load(agree_i[0:1, 0:1], min_val=0, max_val=1)
            with act.If(ok == 0):
                with act.Fori(0, CHUNKS) as c:
                    for p in range(CHUNK):
                        act.wait_ge(seq_pre, c * CHUNK + (p + 1))
                        act.activation(piece[:, p, :], bank[p % 2][:, 0:BATCH], ACT.Tanh).then_inc(seq_state, 1)
                    act.wait_ge(seq_state, c * CHUNK + (CHUNK + 1))
                    act.activation(states[:, MAIN:].rearrange("h (p k) -> h p k", k=COLS)[:, :, bass.ds(c * BATCH, BATCH)],
                                   piece[:], ACT.Copy).then_inc(seq_kept, 1)
                    act.wait_ge(seq_kept, c + 1)
            act.wait_ge(bg_ready, 1)

            def gate(n):
                act.wait_ge(wg_done, n + 1)
                if n >= 2:
                    act.wait_ge(gated_ready, n - 1)
                act.activation(gate_t[:, n % 2, :], bank[2 + n % 2][:, 0:PC], ACT.Tanh, bias=half_bg[:, 0:1], scale=0.5
                               ).then_inc(tanh_ready, 1)

            def shared(n):
                if n < GROUPS * IC:
                    act.wait_ge(up_done, n + 1)
                    if n >= GELUS:
                        act.wait_ge(act_low, n - GELUS + 1)
                    act.activation(gelu[:, n % GELUS, :], bank[n % 2][:], ACT.Gelu, scale=gelu_in).then_inc(gelu_done, 1)
                if n >= 1:
                    m = n - 1
                    g, i = divmod(m, IC)
                    act.wait_ge(gelu_done, m + 1)
                    act.activation(act_hi[:, g, i, :], gelu[:, m % GELUS, :], ACT.Copy, scale=act_scale
                                   ).then_inc(act_high, 1)

            gate(0)
            for s in range(PAIRS + 4):
                if s + 1 < PAIRS:
                    gate(s + 1)
                if 0 <= s - 2 < PAIRS:
                    n = s - 2
                    act.wait_ge(norm2_ready, 2 * n + 2)
                    act.activation(rows[:, 2 * n:2 * n + 2, 0:P], norm2[:, ts4(n), :], ACT.Copy).then_inc(rows_high, 1)
                if s >= 4:
                    n = s - 4
                    act.wait_ge(rows_turned, n + 1)
                    act.activation(x_ffn[:, :, n * PC:(n + 1) * PC],
                                   bank[6][:].bitcast(F16)[:, 0:2 * PC].rearrange("d (h c) -> d h c", h=2), ACT.Copy
                                   ).then_inc(xffn_ready, 1)
                if s == PAIRS:
                    act.wait_ge(w_split, 1)
                    shared(0)
            for n in range(1, GROUPS * IC + 1):
                shared(n)

            def take_turned(k, u):
                act.wait_ge(blk_turned, k + 1)
                act.activation(xblk_t[:, u, :], bank[5][:].bitcast(F16)[:, 0:2 * P], ACT.Copy).then_inc(xt_ready, 1)

            def step(k, v, static, end):
                live = lambda d: static is None or 0 <= static - d < end
                u = v % 2
                if live(0):
                    act.wait_ge(h_done, k * 2 + 1)
                    if static is None or static >= 2:
                        act.wait_ge(prod_ready, k - 1)
                    act.activation(silu[:, u, :], bank[u][:], ACT.Silu, scale=silu_in).then_inc(silu_ready, 1)
                if live(-1):
                    take_turned(k + 1, 1 - u)
                if live(1):
                    act.wait_ge(prod_turned, k)
                    if static is None or static >= 3:
                        act.wait_ge(y_done, k - 2)
                    act.activation(prod_hi[:, 1 - u, :], turned[1 - u][:], ACT.Copy).then_inc(prod_high, 1)

            take_turned(0, 0)
            pipelined(act, step, 1)

        @block.vector
        def _(dve):
            n_step = [0]

            def then_wait(ins):
                n_step[0] += 1
                ins.then_inc(dve_step, 1)
                dve.wait_ge(dve_step, n_step[0])

            dve.memset(states[:, 0:COLS], 0.0).then_inc(state_ready, 1)
            dve.memset(piece[:, CHUNK - 1, :], 0.0).then_inc(seq_state, 1)
            dve.memset(x_in[:].rearrange("h (p k) -> h p k", k=XW)[:, :, 0:PADC], 0.0).then_inc(pads_zero, 1)
            dve.wait_ge(small_in, 80)
            dve.tensor_scalar(half_bg[:], bg_sb[:], 0.5, None, ALU.mult).then_inc(bg_ready, 1)

            dve.tensor_copy(ident16[:], ident).then_inc(ident16_ready, 1)

            def statistics(src, st, mv, ve, tiles, ready, unit=1.0):
                for t in tiles:
                    ins = dve.bn_stats(st[:, t, :], src[:, t, :])
                then_wait(ins)
                for t in tiles:
                    ins = dve.bn_aggr(mv[:, t, :], st[:, t, :])
                then_wait(ins)
                ts = slice(tiles[0], tiles[-1] + 1)
                dve.tensor_scalar(ve[:, ts], mv[:, ts, 1], EPS, unit, ALU.add, ALU.mult).then_inc(ready, 1)

            def normalise(dst, src, mv, rs, tiles, n, ready):
                for i, t in enumerate(tiles):
                    dve.tensor_scalar(dst[:, n % 2 * 2 + i, :], src[:, t, :], mv[:, t, 0:1], rs[:, t:t + 1],
                                      ALU.subtract, ALU.mult).then_inc(ready, 1)

            def greatest(out_col, src):
                return dve.tensor_reduce(out_col, src, AX.X, ALU.max, apply_absolute_value=True)

            def greatest_part(j):
                dve.wait_ge(w_in[j], 16)
                return greatest(part_max[:, j // PARTS, j % PARTS:j % PARTS + 1],
                                (w1_sb, w3_sb, w2_sb)[j // PARTS][:, part(j)])

            for s in range(PAIRS + 2):
                if 0 <= s - 2:
                    n = s - 2
                    dve.wait_ge(rstd_ready, n + 1)
                    normalise(norm_rows, emb_rows, meanvar, rstd, pair_tiles(n), n, norm_ready)
                    p0 = PPT * pair_tiles(n)[0]
                    dve.wait_ge(norm_turned, n + 1)
                    dve.tensor_copy(x_in[:, p0 * XW:(p0 + PPP) * XW].rearrange("h (p k) -> h p k", k=XW)[:, :, PADC:XW],
                                    bank[2 + n % 2][:, 0:PC].rearrange("h (p k) -> h p k", k=COLS)).then_inc(x_ready, 1)
                if s < PAIRS:
                    dve.wait_ge(gathered[s], 32)
                    statistics(emb_rows, stats, meanvar, vareps, pair_tiles(s), var_ready)
                if s == 1:
                    dve.wait_ge(wgc_done, 1)
                    dve.tensor_copy(wgc[:], bank[4][:, 0:P]).then_inc(wgc_ready, 1)
            dve.wait_ge(sh_weights_in, 32)
            greatest(max_rows[:, 3:4], sw1_sb[:])
            greatest(max_rows[:, 4:5], sw2_sb[:])
            greatest(max_rows[:, 5:6], gate_sb[:])
            for j in range(3 * PARTS):
                ins = greatest_part(j)
            then_wait(ins)
            dve.tensor_reduce(max_rows[:, 0:3], part_max[:], AX.X, ALU.max).then_inc(max_ready, 1)
            dve.wait_ge(max_turned, 1)
            then_wait(dve.tensor_reduce(max_col[:], bank[5][0:WEIGHTS, 0:P], AX.X, ALU.max))
            dve.tensor_scalar(max_diag[:], ident[0:WEIGHTS, 0:WEIGHTS], max_col[:], None, ALU.mult).then_inc(diag_ready, 1)
            dve.wait_ge(max_spread, 1)
            then_wait(dve.tensor_copy(max_all[:], bank[6][:, 0:WEIGHTS]))
            then_wait(dve.tensor_scalar(max_exp[:], max_all[:].bitcast(I32), 0x7F800000, None, ALU.bitwise_and))
            then_wait(dve.tensor_scalar(max_exp_in[:], max_exp[:], float(97 << 23), float(167 << 23), ALU.max, ALU.min))
            then_wait(dve.tensor_scalar(scale_i[:], max_exp_in[:], -1.0, float(268 << 23), ALU.mult, ALU.add))
            then_wait(dve.tensor_scalar(unscale_i[:], scale_i[:], -1.0, float(254 << 23), ALU.mult, ALU.add))
            dve.tensor_scalar(silu_in, unscale[:, 0:1], 1 / X_SCALE, None, ALU.mult)
            dve.tensor_scalar(prod_scale, scale[:, 0:1], 2.0 ** -29 / X_SCALE, None, ALU.mult)
            dve.tensor_scalar(gelu_in, unscale[:, 3:4], 1 / X_SCALE, None, ALU.mult)
            dve.tensor_scalar(act_scale, scale[:, 3:4], 2.0 ** -7, None, ALU.mult)
            dve.tensor_tensor(inv_w1w3[:], unscale[:, 0:1], unscale[:, 1:2], ALU.mult)
            then_wait(dve.tensor_tensor(inv_sw[:], unscale[:, 3:4], unscale[:, 4:5], ALU.mult))
            then_wait(dve.tensor_tensor(inv_w1w3w2[:], inv_w1w3[:], unscale[:, 2:3], ALU.mult))
            dve.tensor_scalar(base_unscale, inv_sw[:], 2.0 ** 7, None, ALU.mult)
            dve.tensor_scalar(y_unscale, inv_w1w3w2[:], 2.0 ** 29, None, ALU.mult).then_inc(scales_ready, 1)
            dve.wait_ge(scales_ready, 1)

            for c, w, hl, ready in ((3, sw1_sb, sw1_hl, sh_split), (4, sw2_sb, sw2_hl, sh_split),
                                    (5, gate_sb, gate_hl, sh_split), (0, w1_sb, w1_hl, w_split)):
                then_wait(dve.tensor_scalar(hl[:, 0, :], w[:], scale[:, c:c + 1], None, ALU.mult))
                dve.scalar_tensor_tensor(out=hl[:, 1, :], in0=w[:], scalar=scale[:, c:c + 1], in1=hl[:, 0, :],
                                         op0=ALU.mult, op1=ALU.subtract).then_inc(ready, 1)

            def low_part(lo, hi, w, c, j):
                dve.wait_ge(w_high, (c - 1) * EXPERTS + j + 1)
                ins = dve.scalar_tensor_tensor(out=lo, in0=w, scalar=scale[:, c:c + 1], in1=hi,
                                               op0=ALU.mult, op1=ALU.subtract)
                if j == EXPERTS - 1:
                    ins.then_inc(w_split, 1)

            def w3_low(j):
                cols = slice(j * INNER, (j + 1) * INNER)
                low_part(w3_hl[:, 1, cols], w3_hl[:, 0, cols], w3_sb[:, cols], 1, j)

            def w2_low(j):
                chunks = slice(j * IC, (j + 1) * IC)
                low_part(w2_hl[:, chunks, 1, :], w2_hl[:, chunks, 0, :],
                         w2_sb[:, j * INNER:(j + 1) * INNER].rearrange("i (c d) -> i c d", d=P), 2, j)

            for j in range(EXPERTS - 4):
                w3_low(j)

            met, last = (1 + WARM - MEET) * COLS, (1 + STEPS - MEET) * COLS
            dve.wait_ge(state_ready, 1 + STEPS - MEET)
            then_wait(dve.tensor_tensor(diff[:], states[:, met - COLS + BATCH:met],
                                        states[:, last - COLS:last - BATCH], ALU.subtract))
            then_wait(dve.tensor_tensor(diff2[:], diff[:], diff[:], ALU.mult))
            then_wait(dve.tensor_scalar(close[:], diff2[:], TOL * TOL, None, ALU.is_le))
            dve.tensor_reduce(close_row[:], close[:], AX.X, ALU.min).then_inc(close_ready, 1)
            dve.wait_ge(close_turned, 1)
            then_wait(dve.tensor_reduce(agree[:], bank[2][0:1, 0:P], AX.X, ALU.min))
            dve.tensor_copy(agree_i[:], agree[:]).then_inc(agree_ready, 1)
            for j in range(EXPERTS - 4, EXPERTS):
                w3_low(j)

            for s in range(PAIRS + 2):
                if s < PAIRS:
                    n = s
                    dve.wait_ge(tanh_ready, n + 1)
                    dve.wait_ge(c_done, n + 1)
                    if n >= 2:
                        dve.wait_ge(wo_done, n - 1)
                    dve.scalar_tensor_tensor(out=gated[:, n % 2, :], in0=gate_t[:, n % 2, :], scalar=1.0,
                                             in1=bank[n % 2][:, 0:PC], op0=ALU.add, op1=ALU.mult).then_inc(gated_ready, 1)
                if 0 <= s - 1 < PAIRS:
                    n = s - 1
                    ts = slice(2 * n, 2 * n + 2)
                    dve.wait_ge(wo_done, n + 1)
                    dve.wait_ge(resid_ready, n // 2 + 1)
                    dve.scalar_tensor_tensor(out=attn_out[:, ts, :],
                                             in0=bank[4 + n % 2][:, 0:PC].rearrange("q (t d) -> q t d", t=2),
                                             scalar=0.5, in1=emb_rows[:, ts, :], op0=ALU.mult, op1=ALU.add
                                             ).then_inc(attn_ready, 1)
                if 0 <= s - 2 < PAIRS:
                    n = s - 2
                    dve.wait_ge(rstd2_ready, n + 1)
                    if n >= 2:
                        dve.wait_ge(rows_ready, n - 1)
                    normalise(norm2, attn_out, meanvar2, rstd2, (2 * n, 2 * n + 1), n, norm2_ready)
                if 0 <= s - 1 < PAIRS:
                    n = s - 1
                    dve.wait_ge(attn_ready, n + 1)
                    statistics(attn_out, stats2, meanvar2, vareps2, (2 * n, 2 * n + 1), var2_ready, X_SCALE ** -2)

            def act_low_half(n):
                g, i = divmod(n, IC)
                dve.wait_ge(act_high, n + 1)
                dve.scalar_tensor_tensor(out=act_lo[:, g, i, :], in0=gelu[:, n % GELUS, :], scalar=act_scale,
                                         in1=act_hi[:, g, i, :], op0=ALU.mult, op1=ALU.subtract
                                         ).then_inc(act_low, 1)

            te = lambda ap: ap.rearrange("q (t e) -> q t e", e=EXPERTS)
            et = lambda ap: ap.rearrange("q (e t) -> q t e", e=EXPERTS)
            over = lambda ap: ap.unsqueeze(2).to_broadcast([P, TILES, EXPERTS])
            rev = cst[:, C_REV:C_REV + ET]
            dve.wait_ge(logits_done, 1)
            both = bank[7][:, 0:2 * ET].rearrange("q (t h e) -> q t e h", h=2, e=EXPERTS)
            then_wait(dve.tensor_reduce(te(logits[:]), both, AX.X, ALU.add))
            then_wait(dve.tensor_reduce(top[:], te(logits[:]), AX.X, ALU.max))
            then_wait(dve.tensor_tensor(te(is_top[:]), te(logits[:]), over(top[:]), ALU.is_ge))
            then_wait(dve.tensor_tensor(rev_top[:], is_top[:], rev, ALU.mult))
            then_wait(dve.tensor_reduce(first_rev[:], te(rev_top[:]), AX.X, ALU.max))
            dve.tensor_tensor(et(onehot[:]), te(rev), over(first_rev[:]), ALU.is_equal).then_inc(onehot_ready, 1)
            act_low_half(0)
            dve.wait_ge(counts_done, 1)
            dve.wait_ge(onehot_ready, 1)
            then_wait(dve.tensor_tensor_scan(upto[:], cst[:, C_CARRY:C_CARRY + ET], bank[4][:, 0:ET], 0.0,
                                             ALU.mult, ALU.add))
            counts = upto[:].rearrange("q (e t) -> q e t", e=EXPERTS)[:, :, TILES - 1]
            dve.tensor_scalar(blocks_i0[:], counts, float(P - 1), None, ALU.add)
            then_wait(dve.tensor_tensor(place[:], bank[5][:, 0:ET], upto[:], ALU.add))
            then_wait(dve.tensor_scalar(blocks_i[:], blocks_i0[:], 7, None, ALU.logical_shift_right))
            then_wait(dve.tensor_tensor_scan(blocks_end[:], cst[:, C_ONES:C_ONES + EXPERTS], blocks_i[:], 0.0,
                                             ALU.mult, ALU.add))
            then_wait(dve.tensor_tensor(blocks_start[:], blocks_end[:], blocks_i[:], ALU.subtract))
            e_t = lambda ap: ap.rearrange("q (e t) -> q e t", e=EXPERTS)
            then_wait(dve.scalar_tensor_tensor(out=e_t(place_all[:]),
                                               in0=blocks_start[:].unsqueeze(2).to_broadcast([P, EXPERTS, TILES]),
                                               scalar=float(P), in1=e_t(place[:]), op0=ALU.mult, op1=ALU.add))
            then_wait(dve.tensor_tensor(place_own[:], place_all[:], onehot[:], ALU.mult))
            then_wait(dve.tensor_reduce(slot_f[:], et(place_own[:]), AX.X, ALU.add))
            dve.tensor_copy(slot_i[:], slot_f[:]).then_inc(slots_ready, 1)
            k_e = lambda ap: ap.rearrange("q (k e) -> q k e", e=EXPERTS)
            then_wait(dve.tensor_tensor(k_e(past[:]), k_e(cst[0:1, C_BLOCK:C_BLOCK + BLOCKS * EXPERTS]),
                                        blocks_end[0:1, :].unsqueeze(1).to_broadcast([1, BLOCKS, EXPERTS]), ALU.is_ge))
            then_wait(dve.tensor_reduce(block_expert_f[:], k_e(past[:]), AX.X, ALU.add))
            dve.tensor_scalar(few_blocks[:], blocks_end[0:1, EXPERTS - 1:EXPERTS], float(FEW), None, ALU.is_le)
            dve.tensor_scalar(block_expert[:], block_expert_f[:], float(EXPERTS - 1), None, ALU.min
                              ).then_inc(experts_ready, 1)

            def take_down(g):
                ts = slice(4 * g, 4 * g + 4)
                dve.wait_ge(down_done, g + 1)
                dve.scalar_tensor_tensor(out=attn_out[:, ts, :],
                                         in0=bank[2 + g % 2][:].rearrange("q (t d) -> q t d", t=4),
                                         scalar=base_unscale, in1=attn_out[:, ts, :], op0=ALU.mult, op1=ALU.add
                                         ).then_inc(base_ready, 1)

            for n in range(1, GROUPS * IC):
                act_low_half(n)
                if n - 5 in range(EXPERTS):
                    w2_low(n - 5)
                if n == 3 * IC - 1:
                    take_down(0)
            for g in range(1, GROUPS):
                take_down(g)

            def step(k, v, static, end):
                live = lambda d: static is None or 0 <= static - d < end
                u, w = v % 2, (v - 2) % RING
                if live(0):
                    dve.wait_ge(silu_ready, k + 1)
                    dve.wait_ge(h_done, k * 2 + 2)
                    if static is None or static >= 2:
                        dve.wait_ge(prod_turned, k - 1)
                    dve.scalar_tensor_tensor(out=prod[:, u, :], in0=bank[2 + u][:], scalar=prod_scale, in1=silu[:, u, :],
                                             op0=ALU.mult, op1=ALU.mult).then_inc(prod_ready, 1)

                def out_first():
                    dve.wait_ge(y_done, k - 1)
                    dve.wait_ge(res_in[w], ring_count(k - 2, w))
                    dve.scalar_tensor_tensor(out=out_part[:, u, :], in0=bank[6][:, P:2 * P], scalar=y_unscale,
                                             in1=res_blk[w][:], op0=ALU.mult, op1=ALU.add).then_inc(part_ready, 1)

                def low_half():
                    dve.wait_ge(prod_high, k)
                    dve.tensor_tensor(prod_lo[:, 1 - u, :], turned[1 - u][:], prod_hi[:, 1 - u, :], ALU.subtract
                                      ).then_inc(prod_low, 1)

                if live(2) and live(0):
                    out_first()
                if live(1):
                    low_half()
                if live(2):
                    if not live(0):
                        out_first()
                    dve.wait_ge(part_ready, k - 1)
                    dve.scalar_tensor_tensor(out=out_blk[w][:], in0=bank[6][:, 0:P], scalar=y_unscale,
                                             in1=out_part[:, u, :], op0=ALU.mult, op1=ALU.add).then_inc(outb_ready, 1)

            pipelined(dve, step, 2)


_ARGS = ("tok", "ids", "consts", "emb", "sq", "bg", "bo", "gate", "w1", "w3", "w2", "sw1", "sw2")


def kernel(x, L0_tok_W, L0_attn_A, L0_attn_B, L0_attn_C, L0_attn_Wg, L0_attn_bg, L0_attn_Wo, L0_attn_bo,
           L0_ffn_gate_w, L0_ffn_w1, L0_ffn_w2, L0_ffn_w3, L0_ffn_sw1, L0_ffn_sw2):
    import concourse.bacc as bacc
    from concourse.bass_utils import run_bass_kernel_spmd

    row = np.ascontiguousarray
    tok = np.asarray(x).reshape(BATCH, CHUNKS, TILES, PPT).transpose(3, 1, 0, 2).reshape(P, TILES)
    arrays = {
        "tok": row(tok),
        "ids": row_ids(),
        "consts": shape_constants(),
        "emb": row(np.asarray(L0_tok_W).T),
        "sq": row(np.stack([np.asarray(w).T for w in (L0_attn_A, L0_attn_B, L0_attn_C, L0_attn_Wg, L0_attn_Wo)]
                           + [np.asarray(L0_attn_C)], 1)),
        "bg": row(np.asarray(L0_attn_bg).reshape(P, 1)),
        "bo": row(np.asarray(L0_attn_bo).reshape(1, P)),
        "gate": row(np.asarray(L0_ffn_gate_w).T),
        "w1": row(np.asarray(L0_ffn_w1).transpose(2, 0, 1).reshape(P, EXPERTS * INNER)),
        "w3": row(np.asarray(L0_ffn_w3).transpose(2, 0, 1).reshape(P, EXPERTS * INNER)),
        "w2": row(np.asarray(L0_ffn_w2).reshape(EXPERTS, P, IC, P).transpose(3, 0, 2, 1).reshape(P, EXPERTS * INNER)),
        "sw1": row(np.asarray(L0_ffn_sw1).T),
        "sw2": row(np.asarray(L0_ffn_sw2).reshape(P, IC, P).transpose(2, 1, 0).reshape(P, INNER)),
    }
    nc = bacc.Bacc("TRN2", target_bir_lowering=False, num_devices=1)
    aps = [nc.dram_tensor(n, arrays[n].shape, mybir.dt.from_np(arrays[n].dtype), kind="ExternalInput").ap()
           for n in _ARGS]
    out = nc.dram_tensor("out", (BATCH * SEQ, P), F32, kind="ExternalOutput").ap()
    dispatch = nc.dram_tensor("dispatch", (BLOCKS * P, ROW), F16).ap()
    resid = nc.dram_tensor("resid", (TILES * P, P), F32).ap()
    build(nc, *aps, out, dispatch, resid)
    got = run_bass_kernel_spmd(nc, [arrays], core_ids=[0])
    return got.results[0]["out"].reshape(BATCH, SEQ, P)
```
